# Optimizing a Trainium2 kernel written in Bass

```python
import numpy as np
import jax
import jax.numpy as jnp

def _softmax(x, axis=-1):
    return jax.nn.softmax(x, axis=axis)
def _gelu(x):
    return jax.nn.gelu(x, approximate=True)
def _silu(x):
    return jax.nn.silu(x)
def _sigmoid(x):
    return jax.nn.sigmoid(x)
def _layernorm(x, axis=-1, eps=1e-5):
    m = jnp.mean(x, axis=axis, keepdims=True)
    v = jnp.var(x, axis=axis, keepdims=True)
    return (x - m) / jnp.sqrt(v + eps)
def _scatter_add(tgt, idx, src, axis=0):
    return tgt.at[idx].add(src)
def _segment_sum(src, seg, n):
    return jax.ops.segment_sum(src, seg, n)

kernel_name = 'mk_conv_preact_d1_conv_nhwc64_7823ad'

def setup_inputs(seed: int = 0):
    np.random.seed(seed)
    _w = jnp.asarray
    def _rec_inputs():
        import jax
        import jax.numpy as jnp
        _gk = jax.random.key(seed)
        x = -0.000125 + 0.9999 * jax.random.normal(jax.random.fold_in(_gk, 1), (8, 256, 256, 64), jnp.float32)
        return x
    x = _rec_inputs()
    def _L0_conv_setup():
        import jax, jax.numpy as jnp
        import numpy as np
        N, R, IN_DIM, OUT_DIM, MODE = (8, 256, 64, 64, 32)
        key = jax.random.key(seed)
        k_x, k_w0, k_w1, k_rw, k_rb = jax.random.split(key, 5)
        scale = 1.0 / (IN_DIM * OUT_DIM) * np.sqrt(IN_DIM + OUT_DIM)
        return {'x': jax.random.normal(k_x, (N, R, R, IN_DIM), dtype=jnp.float32), 'w0': jax.random.normal(k_w0, (MODE, MODE, IN_DIM, OUT_DIM, 2), dtype=jnp.float32) * scale, 'w1': jax.random.normal(k_w1, (MODE, MODE, IN_DIM, OUT_DIM, 2), dtype=jnp.float32) * scale, 'res_w': jax.random.normal(k_rw, (IN_DIM, OUT_DIM), dtype=jnp.float32) * 0.05, 'res_b': jax.random.normal(k_rb, (OUT_DIM,), dtype=jnp.float32) * 0.05}
    _L0_conv_all = _L0_conv_setup()
    _L0_conv_in = {k: v for k, v in _L0_conv_all.items() if k in ('w0', 'w1', 'res_w', 'res_b', )}
    del _L0_conv_all

    return {
        "x": x,
        "L0_conv_w0": _L0_conv_in["w0"],
        "L0_conv_w1": _L0_conv_in["w1"],
        "L0_conv_res_w": _L0_conv_in["res_w"],
        "L0_conv_res_b": _L0_conv_in["res_b"],
    }

def reference(x, L0_conv_w0, L0_conv_w1, L0_conv_res_w, L0_conv_res_b):
    import jax
    import jax.numpy as jnp
    def _L0_conv_ref(x, w0, w1, res_w, res_b):
        import jax, jax.numpy as jnp
        import numpy as np
        N, R, IN_DIM, OUT_DIM, MODE = (8, 256, 64, 64, 32)
        n, r, _, in_dim = x.shape
        m = w0.shape[0]
        rc = r // 2 + 1
        out_dim = w0.shape[3]
        res = jnp.einsum('nhwi,io->nhwo', x, res_w) + res_b
        xt = jnp.transpose(x, (0, 3, 1, 2))
        x_ft = jnp.fft.rfft2(xt, s=(r, r), norm='ortho')
        blk0 = x_ft[:, :, :m, :m]
        blk1 = x_ft[:, :, r - m:, :m]
        W0 = w0[..., 0] + 1j * w0[..., 1]
        W1 = w1[..., 0] + 1j * w1[..., 1]
        out0 = jnp.einsum('nixy,xyio->noxy', blk0, W0)
        out1 = jnp.einsum('nixy,xyio->noxy', blk1, W1)
        out_ft = jnp.zeros((n, out_dim, r, rc), dtype=out0.dtype)
        out_ft = out_ft.at[:, :, :m, :m].set(out0)
        out_ft = out_ft.at[:, :, r - m:, :m].set(out1)
        y = jnp.fft.irfft2(out_ft, s=(r, r), norm='ortho')
        y = jnp.transpose(y, (0, 2, 3, 1))
        return jax.nn.silu(y + res)

    def _gn(v, G=32, eps=1e-5):
        B_, H_, W_, C_ = v.shape
        g = v.reshape(B_, H_, W_, G, C_ // G)
        m = jnp.mean(g, axis=(1, 2, 4), keepdims=True)
        s = jnp.var(g, axis=(1, 2, 4), keepdims=True)
        return ((g - m) / jnp.sqrt(s + eps)).reshape(v.shape)

    def _ln_c(v, eps=1e-6):
        m = jnp.mean(v, axis=-1, keepdims=True)
        s = jnp.var(v, axis=-1, keepdims=True)
        return (v - m) / jnp.sqrt(s + eps)

    def _ln_t(v, eps=1e-5):
        m = jnp.mean(v, axis=-1, keepdims=True)
        s = jnp.var(v, axis=-1, keepdims=True)
        return (v - m) / jnp.sqrt(s + eps)

    def _to_tokens(v):
        B_, H_, W_, C_ = v.shape
        return v.reshape(B_, H_ * W_, C_)
    def _from_tokens(t, like):
        return t.reshape(like.shape)

    x = x + _L0_conv_ref(_gn(x), L0_conv_w0, L0_conv_w1, L0_conv_res_w, L0_conv_res_b)
    return x


_drawn_inputs = setup_inputs


def setup_inputs(seed=0):
    import zlib

    import numpy as np

    out = dict(_drawn_inputs(seed))
    spreads = {}
    factors = {'L0_conv_w0': 8.0, 'L0_conv_w1': 8.0}
    for name, (base, spread) in spreads.items():
        noise = np.random.default_rng([zlib.crc32(name.encode()), seed]).standard_normal(out[name].shape)
        drawn = base * np.exp(spread * noise) if base else spread * noise
        out[name] = jnp.asarray(drawn.astype(out[name].dtype))
    for name, factor in factors.items():
        out[name] = (out[name] * factor).astype(out[name].dtype)
    return out
```

```python
from contextlib import ExitStack

import numpy as np
import concourse.bass as bass
from concourse import mybir

N, R, C, MODE = 8, 256, 64, 32
P = 128
KW, KH = MODE, 2 * MODE
KP = KW // 2
GROUPS, EPS = 32, 1e-5
CHUNK = 16
CHUNKS = R // CHUNK
HALF = CHUNK // 2
ROW = 2 * C
CELL = CHUNK * ROW
XSLOTS = 8
BANK = 512
STATROWS = 64
MACROS = R // STATROWS
PER_MACRO = STATROWS // CHUNK
FILLS = C // 4
GK = KW // 4
AFILLS = C // 4
UNITS = R // HALF
OSLOTS = 4

T_FW, T_GH, T_EH, T_EW, T_ID, T_MASK = 0, 128, 640, 1152, 1664, 1792
T_ALL = 1824


def constant_table():
    t = np.zeros((P, T_ALL))
    w = 2 * np.arange(P)[:, None] + np.arange(2)[None, :]
    kw = np.arange(KW)
    a = 2 * np.pi * w[:, :, None] * kw / R
    t[:, T_FW:T_GH] = (np.stack([np.cos(a), -np.sin(a)], 2) / R).reshape(P, -1)
    kh = np.concatenate([np.arange(MODE), np.arange(R - MODE, R)])
    q = np.arange(P)
    h = (q // HALF)[:, None] * CHUNK + np.arange(2)[None, :] * HALF + (q % HALF)[:, None]
    b = 2 * np.pi * ((h[:, :, None] * kh) % R) / R
    g = np.stack([np.stack([np.cos(b), -np.sin(b)], 2), np.stack([np.sin(b), np.cos(b)], 2)], 2)
    t[:, T_GH:T_EH] = g.reshape(P, -1)
    d = 2 * np.pi * ((kh[:, None] * np.arange(R)) % R) / R
    e = np.stack([np.stack([np.cos(d), np.sin(d)], 1), np.stack([-np.sin(d), np.cos(d)], 1)], 0)
    t[:, T_EH:T_EW] = e.reshape(P, -1)
    order = np.array([GK * tt + gk for gk in range(GK) for tt in range(4)])
    f = 2 * np.pi * order[:, None, None] * w.T[None] / R
    s = np.where(order == 0, 1.0, 2.0)[:, None, None] / R
    ew = np.concatenate([s * np.cos(f), -s * np.sin(f)], 0)
    full = np.zeros((2, 2 * KW, 2, 2, P))
    for o in range(2):
        full[o, :, :, o, :] = ew
    t[:, T_EW:T_ID] = full.reshape(P, -1)
    t[:, T_ID:T_MASK] = np.eye(P)
    t[:, T_MASK:] = (q[:, None] % C) // (C // GROUPS) == np.arange(GROUPS)
    return t.astype(np.float32)


def spectral_layer(nc, x, w0, w1, res_w, res_b, table, out):
    fp32 = mybir.dt.float32
    ALU = mybir.AluOpType
    ACT = mybir.ActivationFunctionType
    AX = mybir.AxisListType
    ds = bass.ds

    x_rows = x.rearrange("n h (p two) c -> p (n h) (two c)", two=2)
    out_rows = out.rearrange("n h (p two) c -> p (n h) (two c)", two=2)
    w0_rows = w0.rearrange("x (q two) i o r -> (two i) x q (o r)", two=2)
    w1_rows = w1.rearrange("x (q two) i o r -> (two i) x q (o r)", two=2)
    mixed = nc.dram_tensor("mixed_modes", [KH, P, 4 * C], fp32).ap()
    mixed_in = mixed.rearrange("k p f -> p k f")
    mixed_out = mixed.rearrange("k (g n r) f -> n r k g f", g=GK, n=N)

    with ExitStack() as ctx:
        def sb(name, shape):
            return ctx.enter_context(nc.sbuf_tensor(name, shape, fp32))

        def sem(name):
            return ctx.enter_context(nc.semaphore(name))

        ring = sb("ring", [P, XSLOTS, CELL])
        work = sb("work", [P, 2, C * P])
        spectrum = sb("spectrum", [P, KH, KP, N, 2])
        const = sb("const", [P, T_ALL])
        ones = sb("ones", [P, P])
        w_block = sb("w_block", [P, P])
        w_scaled = sb("w_scaled", [P, P])
        cells = sb("cells", [P, MACROS, GROUPS, 6])
        spread = sb("spread", [P, MACROS, GROUPS, 2])
        sums = sb("sums", [P, GROUPS])
        mean = sb("mean", [P, GROUPS])
        rstd = sb("rstd", [P, GROUPS])
        var = sb("var", [P, GROUPS])
        root = sb("root", [P, GROUPS])
        picked = sb("picked", [P, GROUPS])
        chan = sb("chan", [P, 4])
        scale_all = sb("scale_all", [P, N])
        shift_all = sb("shift_all", [P, N])
        dc_all = sb("dc_all", [P, N])
        now = sb("now", [P, 2])
        bias = sb("bias", [1, 2 * C])
        spare = sb("spare", [P, 4])

        psum = ctx.enter_context(nc.psum_tensor("psum", [P, 8, BANK], fp32))

        fw = const[:, T_FW:T_GH].rearrange("p (two m) -> p two m", two=2)
        gh = const[:, T_GH:T_EH].rearrange("p (a r m) -> p a r m", a=2, r=2)
        eh = const[:, T_EH:T_EW].rearrange("p (r h) -> p r h", r=2)
        ew = const[:, T_EW:T_ID].rearrange("p (two o m) -> p two o m", two=2, o=2)
        ident = const[:, T_ID:T_MASK]
        mask = const[:, T_MASK:T_ALL]

        x_slot = [ring[:, s, :].rearrange("p (h f) -> p h f", f=ROW) for s in range(XSLOTS)]
        w_slot = [ring[:, s, :].rearrange("p (q o r) -> p q o r", q=KP, r=2) for s in range(XSLOTS)]
        rows_w = work[:, 0, :].rearrange("p (c h) -> p c h", c=C)
        rows_h = work[:, 1, :].rearrange("p (m c) -> p m c", c=C)
        blocks = work[:, 0, 0:4 * KP * 2 * 2 * N * 2].rearrange(
            "p (b q v k n r) -> p b q v k n r", b=4, q=KP, v=2, k=2, n=N)
        mix_out = work[:, 1, 0:4 * 2 * 4 * C].rearrange("p (m k f) -> p m k f", m=4, k=2)
        o_slot = [work[:, 0, s * CELL:(s + 1) * CELL].rearrange("p (h f) -> p h f", f=ROW) for s in range(OSLOTS)]
        flat = spectrum[:, :, :, :, :].rearrange("p a b c d -> p (a b c d)")
        a_all = flat[:, 0:R * 32].rearrange("p (h o) -> p h o", o=32)
        modes = flat[:, R * 32:R * 32 + KW * C].rearrange("p (k o) -> p k o", o=C)
        xt0 = R * 32 + KW * C
        xt = [flat[:, xt0 + b * 2 * BANK:xt0 + (b + 1) * 2 * BANK] for b in range(2)]

        consts_loaded = sem("consts_loaded")
        w_cleared = sem("w_cleared")
        res_loaded = sem("res_loaded")
        ones_set = sem("ones_set")
        x1_loaded = [sem(f"x1_loaded{s}") for s in range(XSLOTS)]
        fw_done = sem("fw_done")
        rows_w_copied = sem("rows_w_copied")
        turned = sem("turned")
        rows_h_copied = sem("rows_h_copied")
        fh_done = sem("fh_done")
        spectrum_copied = sem("spectrum_copied")
        stats_done = sem("stats_done")
        dve_step = sem("dve_step")
        sums_ready = sem("sums_ready")
        totals_ready = sem("totals_ready")
        totals_read = sem("totals_read")
        var_ready = sem("var_ready")
        root_ready = sem("root_ready")
        chan_ready = sem("chan_ready")
        blocks_cleared = sem("blocks_cleared")
        w_loaded = [sem(f"w_loaded{s}") for s in range(XSLOTS)]
        blocks_ready = sem("blocks_ready")
        mix_done = sem("mix_done")
        mix_banks = sem("mix_banks")
        mixed_stored = [sem(f"mixed_stored{m}") for m in range(4)]
        modes_loaded = sem("modes_loaded")
        shift_ready = sem("shift_ready")
        shift_summed = sem("shift_summed")
        modes_ready = sem("modes_ready")
        ih_done = sem("ih_done")
        a_by_act = sem("a_by_act")
        a_by_dve = sem("a_by_dve")
        x2_loaded = [sem(f"x2_loaded{s}") for s in range(OSLOTS)]
        xt_done = sem("xt_done")
        xt_banks = sem("xt_banks")
        z_done = sem("z_done")
        z_banks = sem("z_banks")
        added = sem("added")
        stored = [sem(f"stored{s}") for s in range(OSLOTS)]

        block = ctx.enter_context(nc.Block())

        @block.sync
        def _(sp):
            sp.dma_start(const[:, :], table).then_inc(consts_loaded, 16)
            for s in range(4):
                for free in (stored[s], mixed_stored[s]):
                    sp.dma_start(spare[0:1, 2:3], table[0:1, 0:1]).then_inc(free, 16)
                    sp.wait_ge(free, 16)
            sp.wait_ge(w_cleared, 1)
            for b in range(2):
                sp.dma_start(w_block[b * C:(b + 1) * C, b * C:(b + 1) * C], res_w).then_inc(res_loaded, 16)
            sp.dma_start(bias[0:1, 0:C], res_b.rearrange("(a o) -> a o", a=1)).then_inc(res_loaded, 16)

            def load_x(s, row, loaded):
                for part in range(2):
                    sp.dma_start(x_slot[s][:, HALF * part:HALF * (part + 1), :],
                                 x_rows[:, ds(row + HALF * part, HALF), :]).then_inc(loaded[s], 16)

            for s in range(XSLOTS):
                load_x(s, s * CHUNK, x1_loaded)

            def refill(n, macro):
                chunks = sp.snap(CHUNKS * n + PER_MACRO * (macro + 1))
                sp.wait_ge(stats_done, chunks)
                sp.wait_ge(fw_done, chunks)
                for j in range(PER_MACRO):
                    s = (macro % 2) * PER_MACRO + j
                    load_x(s, R * n + STATROWS * (macro + 2) + CHUNK * j, x1_loaded)

            with sp.Fori(0, N - 1) as n:
                for macro in range(MACROS):
                    refill(n, macro)
            for macro in range(MACROS - 2):
                refill(N - 1, macro)

            def load_weights(s, it):
                rows = w0_rows if s < 4 else w1_rows
                for part in range(2):
                    sp.dma_start(ring[:, s, part * CELL // 2:(part + 1) * CELL // 2].rearrange(
                                     "p (a q f) -> p a q f", a=1, f=2 * C),
                                 rows[:, ds(4 * it + s % 4, 1), part * KP // 2:(part + 1) * KP // 2, :]
                                 ).then_inc(w_loaded[s], 16)

            for macro in range(2):
                sp.wait_ge(stats_done, CHUNKS * (N - 1) + PER_MACRO * (MACROS - 1 + macro))
                sp.wait_ge(fw_done, CHUNKS * (N - 1) + PER_MACRO * (MACROS - 1 + macro))
                for s in range(4 * macro, 4 * macro + 4):
                    load_weights(s, 0)
            with sp.Fori(0, 7) as it:
                for s in range(XSLOTS):
                    sp.wait_ge(mix_done, 4 + 8 * it + s + 1)
                    load_weights(s, it + 1)

            for s in range(OSLOTS):
                sp.wait_ge(mix_done, 4 + KH - 8 + s + 1)
                load_x(s, s * CHUNK, x2_loaded)
            with sp.Fori(0, N * CHUNKS // OSLOTS - 1) as four:
                for s in range(OSLOTS):
                    sp.wait_ge(added, OSLOTS * four + s + 1)
                    load_x(s, CHUNK * (OSLOTS * four + s + OSLOTS), x2_loaded)
                    sp.dma_start(out_rows[:, ds(CHUNK * (OSLOTS * four + s), CHUNK), :], o_slot[s]
                                 ).then_inc(stored[s], 16)
            last = N * CHUNKS - OSLOTS
            for s in range(OSLOTS):
                sp.wait_ge(added, last + s + 1)
                sp.dma_start(out_rows[:, CHUNK * (last + s):CHUNK * (last + s + 1), :], o_slot[s]
                             ).then_inc(stored[s], 16)
            for s in range(OSLOTS):
                sp.wait_ge(stored[s], 16 * (N * CHUNKS // OSLOTS + 1))

        @block.gpsimd
        def _(pool):
            pool.memset(w_block[:, :], 0.0).then_inc(w_cleared, 1)
            pool.memset(ones[:, :], 1.0).then_inc(ones_set, 1)
            for m in range(4):
                pool.wait_ge(mixed_stored[m], 16 * 9)

            def load_modes(n):
                for ri in range(2):
                    pool.dma_start(modes[ri * KH:(ri + 1) * KH].rearrange("p (g t) o -> p g (t o)", t=4),
                                   mixed_out[n, ri]).then_inc(modes_loaded, 16)

            load_modes(0)
            with pool.Fori(0, N - 1) as n:
                pool.wait_ge(ih_done, AFILLS * (n + 1))
                load_modes(n + 1)

        @block.scalar
        def _(act):
            act.wait_ge(consts_loaded, 16)
            nc.scalar.copy(spare[:, 0:1], const[:, 0:1]).then_inc(mix_banks, 4)
            nc.scalar.copy(spare[:, 1:2], const[:, 0:1]).then_inc(z_banks, 2)

            with act.Fori(0, N) as n:
                for k in range(CHUNKS):
                    act.wait_ge(fw_done, CHUNKS * n + k + 1)
                    nc.scalar.copy(rows_w[:, :, HALF * k:HALF * (k + 1)],
                                   psum[:, k % 2, :].rearrange("p (h c) -> p c h", c=C)).then_inc(rows_w_copied, 1)
                for f in range(FILLS):
                    act.wait_ge(turned, FILLS * n + f + 1)
                    nc.scalar.copy(rows_h[:, :, 4 * f:4 * f + 4],
                                   psum[:, 2 + f % 2, :].rearrange("p (c m) -> p m c", c=4)).then_inc(rows_h_copied, 1)
                act.wait_ge(var_ready, n + 1)
                nc.scalar.activation(root[:, :], var[:, :], ACT.Sqrt).then_inc(root_ready, 1)
                act.wait_ge(fh_done, 4 * (n + 1))
                act.wait_ge(chan_ready, n + 1)
                for b in range(4):
                    nc.scalar.activation(spectrum[:, :, 4 * b:4 * b + 4, n, :].rearrange("p k q r -> p q r k"),
                                         psum[:, 4 + b, :].rearrange("p (q r k) -> p q r k", q=4, r=2),
                                         ACT.Identity, scale=chan[:, 0:1]).then_inc(spectrum_copied, 1)

            def mix_copy(it, m):
                act.wait_ge(mix_done, 4 + 8 * it + 2 * m + 2)
                act.wait_ge(mixed_stored[m], 16 * (it + 1))
                nc.scalar.copy(mix_out[:, m, :, :], psum[:, m, :].rearrange("p (k f) -> p k f", k=2)
                               ).then_inc(mix_banks, 1)
                act.wait_ge(mix_banks, 4 + 4 * it + m + 1)
                kh = 4 * it + 2 * m if m < 2 else 4 * it + MODE + 2 * (m - 2)
                act.dma_start(mixed_in[:, ds(kh, 2), :], mix_out[:, m, :, :]).then_inc(mixed_stored[m], 16)

            with act.Fori(0, 8) as it:
                for m in range(4):
                    mix_copy(it, m)

            def silu(n, it, v):
                unit = UNITS * n + 8 * it + v
                s = v // 2
                if v % 2 == 0:
                    act.wait_ge(stored[s], 16 * (4 * n + it + 1))
                act.wait_ge(z_done, unit + 1)
                bank = 2 * (v % 2)
                nc.scalar.activation(
                    o_slot[s][:, HALF * (v % 2):HALF * (v % 2 + 1), :],
                    psum[:, bank:bank + 2, :].rearrange("p b (h f) -> p (b h) f", f=ROW),
                    ACT.Silu).then_inc(z_banks, 1)

            with act.Fori(0, N) as n:
                for f in range(0, AFILLS, 2):
                    act.wait_ge(ih_done, AFILLS * n + f + 1)
                    nc.scalar.copy(a_all[:, :, 2 * f:2 * f + 2],
                                   psum[:, f % 4, :].rearrange("p (o h) -> p h o", o=2)).then_inc(a_by_act, 1)
                with act.Fori(0, 4) as it:
                    for v in range(8):
                        silu(n, it, v)

        @block.vector
        def _(dve):
            dve.wait_ge(res_loaded, 48)
            nc.vector.tensor_scalar(bias[0:1, 0:C], bias[0:1, 0:C], float(R), None, ALU.mult).then_inc(xt_banks, 2)
            dve.wait_ge(consts_loaded, 16)

            steps = [0]
            STEPS = 14

            def step(n, ins):
                steps[0] += 1
                ins.then_inc(dve_step, 1)
                dve.wait_ge(dve_step, STEPS * n + steps[0])

            means = cells[:, :, :, 1:5:3]
            moments = cells[:, :, :, 2:6:3]
            with dve.Fori(0, N) as n:
                for macro in range(MACROS):
                    for j in range(PER_MACRO):
                        dve.wait_ge(x1_loaded[(macro % 2) * PER_MACRO + j], 32 * (2 * n + macro // 2 + 1))
                    s = (macro % 2) * PER_MACRO
                    rows = ring[:, s:s + PER_MACRO, :].rearrange("p s (h two c) -> p (s h) two c", two=2, c=C)
                    for g in range(GROUPS):
                        ins = nc.vector.bn_stats(cells[:, macro, g, :], rows[:, :, :, 2 * g:2 * g + 2])
                    ins.then_inc(stats_done, PER_MACRO)
                dve.wait_ge(stats_done, CHUNKS * (n + 1))
                nc.vector.tensor_reduce(sums[:, :], means.rearrange("p m g s -> p g m s"), AX.XY, ALU.add
                                        ).then_inc(sums_ready, 1)
                dve.wait_ge(totals_ready, 2 * n + 1)
                step(n, nc.vector.tensor_scalar(mean[:, :], psum[:, 2, 0:GROUPS],
                                                1.0 / (P * MACROS * 2), None, ALU.mult))
                step(n, nc.vector.tensor_tensor(
                    spread[:, :, :, :], means,
                    mean[:, :].rearrange("p (a g b) -> p a g b", a=1, b=1).to_broadcast([P, MACROS, GROUPS, 2]),
                    ALU.subtract))
                step(n, nc.vector.tensor_tensor(spread[:, :, :, :], spread[:, :, :, :], spread[:, :, :, :], ALU.mult))
                step(n, nc.vector.scalar_tensor_tensor(spread[:, :, :, :], spread[:, :, :, :],
                                                       float(STATROWS * 2), moments, ALU.mult, ALU.add))
                nc.vector.tensor_reduce(sums[:, :], spread[:, :, :, :].rearrange("p m g s -> p g m s"), AX.XY, ALU.add
                                        ).then_inc(sums_ready, 1)
                dve.wait_ge(totals_ready, 2 * n + 2)
                nc.vector.tensor_scalar(var[:, :], psum[:, 3, 0:GROUPS], 1.0 / (R * R * (C // GROUPS)), EPS,
                                        ALU.mult, ALU.add).then_inc(var_ready, 1)
                dve.wait_ge(root_ready, n + 1)
                step(n, nc.vector.reciprocal(rstd[:, :], root[:, :]))
                step(n, nc.vector.tensor_tensor(root[:, :], rstd[:, :], rstd[:, :], ALU.mult))
                step(n, nc.vector.tensor_tensor(root[:, :], root[:, :], var[:, :], ALU.mult))
                step(n, nc.vector.tensor_scalar(root[:, :], root[:, :], -0.5, 1.5, ALU.mult, ALU.add))
                step(n, nc.vector.tensor_tensor(rstd[:, :], rstd[:, :], root[:, :], ALU.mult))
                step(n, nc.vector.tensor_tensor(picked[:, :], rstd[:, :], mask, ALU.mult))
                step(n, nc.vector.tensor_reduce(chan[:, 0:1], picked[:, :], AX.X, ALU.add))
                step(n, nc.vector.tensor_tensor(picked[:, :], mean[:, :], mask, ALU.mult))
                step(n, nc.vector.tensor_reduce(chan[:, 1:2], picked[:, :], AX.X, ALU.add))
                step(n, nc.vector.tensor_tensor(chan[:, 2:3], chan[:, 0:1], chan[:, 1:2], ALU.mult))
                nc.vector.tensor_scalar(scale_all[:, ds(n, 1)], chan[:, 0:1], 1.0, None, ALU.mult)
                nc.vector.tensor_scalar(shift_all[:, ds(n, 1)], chan[:, 2:3], 1.0, None, ALU.mult)
                nc.vector.tensor_scalar(dc_all[:, ds(n, 1)], chan[:, 2:3], -float(R), None, ALU.mult
                                        ).then_inc(chan_ready, 1)
                assert steps[0] == STEPS

            dve.wait_ge(fh_done, 4 * N)
            dve.wait_ge(rows_h_copied, FILLS * N)
            nc.vector.memset(blocks.rearrange("p b q v k n r -> p (b q v k n r)"), 0.0).then_inc(blocks_cleared, 1)
            dve.wait_ge(spectrum_copied, 4 * N)
            nc.vector.tensor_tensor(spectrum[0:C, 0, 0, :, 0], spectrum[0:C, 0, 0, :, 0], dc_all[0:C, :], ALU.add
                                    ).then_inc(blocks_cleared, 1)
            dve.wait_ge(blocks_cleared, 2)
            with dve.Fori(0, 8) as it:
                for s in range(8):
                    dve.wait_ge(mix_done, 8 * it + s + 1)
                    kh = 4 * it + s if s < 4 else 4 * it + MODE + s - 4
                    for half in range(2):
                        rows = slice(C * half, C * (half + 1))
                        z = spectrum[rows, kh, :, :, :]
                        b = blocks[rows, s % 4, :, :, half, :, :]
                        nc.vector.tensor_scalar(b[:, :, 0], z, 1.0, None, ALU.mult)
                        nc.vector.tensor_scalar(b[:, :, 1, :, 0], z[:, :, :, 1], -1.0, None, ALU.mult)
                        ins = nc.vector.tensor_scalar(b[:, :, 1, :, 1], z[:, :, :, 0], 1.0, None, ALU.mult)
                    ins.then_inc(blocks_ready, 1)

            def xt_copy(n, it, v):
                dve.wait_ge(xt_done, UNITS * n + 8 * it + v + 1)
                nc.vector.tensor_copy(xt[v % 2].rearrange("p (b f) -> p b f", b=2),
                                      psum[:, 4 + 2 * (v % 2):6 + 2 * (v % 2), :]).then_inc(xt_banks, 1)

            def add_x(n, it, v):
                dve.wait_ge(z_banks, UNITS * n + 8 * it + v + 3)
                rows = slice(HALF * (v % 2), HALF * (v % 2 + 1))
                s = v // 2
                ins = nc.vector.tensor_tensor(o_slot[s][:, rows, :], o_slot[s][:, rows, :], x_slot[s][:, rows, :],
                                              ALU.add)
                if v % 2:
                    ins.then_inc(added, 1)

            def units(n, it, last):
                for v in range(8):
                    if not (last and v == 7):
                        xt_copy(n, it, v + 1) if v < 7 else xt_copy(n, it + 1, 0)
                    add_x(n, it, v)

            with dve.Fori(0, N) as n:
                xt_copy(n, 0, 0)
                nc.vector.tensor_scalar(now[:, 0:1], scale_all[:, ds(n, 1)], 1.0, None, ALU.mult)
                nc.vector.tensor_scalar(now[:, 1:2], shift_all[:, ds(n, 1)], 1.0, None, ALU.mult).then_inc(shift_ready, 1)
                dve.wait_ge(shift_ready, n + 1)
                nc.vector.tensor_scalar(w_scaled[:, :], w_block[:, :], now[:, 0:1], None, ALU.mult)
                dve.wait_ge(shift_summed, n + 1)
                nc.vector.scalar_tensor_tensor(bias[0:1, C:2 * C], psum[0:1, 0, 0:C], -float(R), bias[0:1, 0:C],
                                               ALU.mult, ALU.add).then_inc(dve_step, 1)
                dve.wait_ge(dve_step, STEPS * N + n + 1)
                dve.wait_ge(modes_loaded, 32 * (n + 1))
                nc.vector.tensor_tensor(modes[0:1, 0, :], modes[0:1, 0, :], bias[0:1, C:2 * C], ALU.add
                                        ).then_inc(modes_ready, 1)
                for f in range(1, AFILLS, 2):
                    dve.wait_ge(ih_done, AFILLS * n + f + 1)
                    nc.vector.tensor_copy(a_all[:, :, 2 * f:2 * f + 2],
                                          psum[:, f % 4, :].rearrange("p (o h) -> p h o", o=2)).then_inc(a_by_dve, 1)
                with dve.Fori(0, 3) as it:
                    units(n, it, False)
                units(n, 3, True)

        @block.tensor
        def _(pe):
            pe.wait_ge(consts_loaded, 16)
            pe.wait_ge(ones_set, 1)
            nc.tensor.matmul(psum[:, 0, 0:P], ones[:, :], ones[:, :], start=True, stop=True).then_inc(mix_done, 4)

            def total(n, which):
                pe.wait_ge(sums_ready, 2 * n + which + 1)
                nc.tensor.matmul(psum[:, 2 + which, 0:GROUPS], ones[:, :], sums[:, :], start=True, stop=True
                                 ).then_inc(totals_ready, 1)

            with pe.Fori(0, N) as n:
                for k in range(CHUNKS):
                    if k >= 2:
                        pe.wait_ge(rows_w_copied, CHUNKS * n + k - 1)
                    pe.wait_ge(x1_loaded[k % XSLOTS], 32 * (2 * n + k // XSLOTS + 1))
                    for two in range(2):
                        for half in range(2):
                            ins = nc.tensor.matmul(
                                psum[half * C:(half + 1) * C, k % 2, :], fw[:, two, :],
                                x_slot[k % XSLOTS][:, HALF * half:HALF * (half + 1), two * C:(two + 1) * C],
                                start=two == 0, stop=two == 1)
                    ins.then_inc(fw_done, 1)
                pe.wait_ge(rows_w_copied, CHUNKS * (n + 1))
                for f in range(FILLS):
                    if f >= 2:
                        pe.wait_ge(rows_h_copied, FILLS * n + f - 1)
                    for c in range(4):
                        ins = nc.tensor.transpose(psum[:, 2 + f % 2, c * P:(c + 1) * P], rows_w[:, 4 * f + c, :], ident)
                    ins.then_inc(turned, 1)
                pe.wait_ge(rows_h_copied, FILLS * (n + 1))
                for q in range(KP):
                    for half in range(2):
                        for ri in range(2):
                            for odd in range(2):
                                m = half * 2 * KW + ri * KW + 2 * q + odd
                                ins = nc.tensor.matmul(psum[odd * C:(odd + 1) * C, 4 + q // 4, (q % 4) * P:(q % 4 + 1) * P],
                                                       rows_h[:, m, :], gh[:, half, ri, :],
                                                       start=(half, ri) == (0, 0), stop=(half, ri) == (1, 1))
                    if q % 4 == 3:
                        ins.then_inc(fh_done, 1)
                    if q in (0, 4):
                        total(n, q // 4)

            with pe.Fori(0, 8) as it:
                for s in range(8):
                    pe.wait_ge(blocks_ready, 8 * it + s + 1)
                    pe.wait_ge(w_loaded[s], 32 * (it + 1))
                    if s % 2 == 0:
                        pe.wait_ge(mix_banks, 4 * it + s // 2 + 1)
                    for t in range(4):
                        for v in range(2):
                            for g in range(4):
                                ins = nc.tensor.matmul(
                                    psum[32 * g:32 * (g + 1), s // 2, (4 * (s % 2) + t) * C:(4 * (s % 2) + t + 1) * C],
                                    blocks[:, s % 4, 4 * t + g, v, :, :, :].rearrange("p k n r -> p (k n r)"), w_slot[s][:, 4 * t + g, :, v],
                                    start=v == 0, stop=v == 1)
                    ins.then_inc(mix_done, 1)

            def transpose_x(n, it, v):
                s = v // 2
                if v % 2 == 0:
                    pe.wait_ge(x2_loaded[s], 32 * (4 * n + it + 1))
                pe.wait_ge(xt_banks, UNITS * n + 8 * it + v + 1)
                for row in range(HALF):
                    ins = nc.tensor.transpose(psum[:, 4 + 2 * (v % 2) + row // 4, (row % 4) * P:(row % 4 + 1) * P],
                                              x_slot[s][:, HALF * (v % 2) + row, :], ident)
                ins.then_inc(xt_done, 1)

            def sum_unit(n, it, v):
                pe.wait_ge(xt_banks, UNITS * n + 8 * it + v + 3)
                pe.wait_ge(z_banks, UNITS * n + 8 * it + v + 1)
                if v == 0:
                    pe.wait_ge(a_by_act, AFILLS // 2 * (n + 1))
                    pe.wait_ge(a_by_dve, AFILLS // 2 * (n + 1))
                for four in range(2):
                    row = HALF * (8 * it + v) + 4 * four
                    z = psum[:, 2 * (v % 2) + four, :].rearrange("p (h two o) -> p h two o", two=2, o=C)
                    for two in range(2):
                        for o in range(2):
                            nc.tensor.matmul(z[:, :, two, 32 * o:32 * (o + 1)], ew[:, two, o, :],
                                             a_all[:, ds(row, 4), :], start=(two, o) == (0, 0), stop=False,
                                             skip_group_check=True)
                    for h in range(4):
                        c0 = (4 * four + h) * P
                        ins = nc.tensor.matmul(z[:, h, :, :], xt[v % 2][:, c0:c0 + P], w_scaled[:, :],
                                               start=False, stop=h == 3, skip_group_check=True)
                ins.then_inc(z_done, 1)

            def units(n, it, last):
                for v in range(8):
                    if not (last and v == 7):
                        transpose_x(n, it, v + 1) if v < 7 else transpose_x(n, it + 1, 0)
                    sum_unit(n, it, v)

            pe.wait_ge(mix_banks, 4 + 4 * 8)
            with pe.Fori(0, N) as n:
                transpose_x(n, 0, 0)
                pe.wait_ge(shift_ready, n + 1)
                pe.wait_ge(z_banks, UNITS * n + 2)
                nc.tensor.matmul(psum[0:1, 0, 0:C], now[:, 1:2], w_block[:, 0:C], start=True, stop=True
                                 ).then_inc(shift_summed, 1)
                pe.wait_ge(modes_ready, n + 1)
                for f in range(AFILLS):
                    if f >= 4:
                        if f % 2 == 0:
                            pe.wait_ge(a_by_act, AFILLS // 2 * n + (f - 4) // 2 + 1)
                        else:
                            pe.wait_ge(a_by_dve, AFILLS // 2 * n + (f - 4) // 2 + 1)
                    for o in range(2):
                        for half in range(2):
                            for ri in range(2):
                                tile = 2 * half + ri
                                ins = nc.tensor.matmul(psum[32 * tile:32 * (tile + 1), f % 4, o * R:(o + 1) * R],
                                                       modes[:, :, 32 * half + 2 * f + o], eh[:, ri, :],
                                                       start=True, stop=True)
                    ins.then_inc(ih_done, 1)
                with pe.Fori(0, 3) as it:
                    units(n, it, False)
                units(n, 3, True)


def kernel(x, L0_conv_w0, L0_conv_w1, L0_conv_res_w, L0_conv_res_b):
    import concourse.bacc as bacc
    from concourse.bass_utils import run_bass_kernel_spmd

    nc = bacc.Bacc("TRN2", target_bir_lowering=False, num_devices=1)
    arrays, args = {}, []
    for name, a in (("x", x), ("w0", L0_conv_w0), ("w1", L0_conv_w1), ("res_w", L0_conv_res_w),
                    ("res_b", L0_conv_res_b), ("table", constant_table())):
        a = np.ascontiguousarray(a)
        arrays[name] = a
        args.append(nc.dram_tensor(name, a.shape, mybir.dt.from_np(a.dtype), kind="ExternalInput").ap())
    out = nc.dram_tensor("out", (N, R, R, C), mybir.dt.float32, kind="ExternalOutput").ap()
    spectral_layer(nc, *args, out)
    return run_bass_kernel_spmd(nc, [arrays], core_ids=[0]).results[0]["out"]
```

```python
from contextlib import ExitStack

import numpy as np
import concourse.bass as bass
from concourse import mybir

N, R, C, MODE = 8, 256, 64, 32
P = 128
KW, KH = MODE, 2 * MODE
KP = KW // 2
GROUPS, EPS = 32, 1e-5
CHUNK = 16
CHUNKS = R // CHUNK
HALF = CHUNK // 2
ROW = 2 * C
CELL = CHUNK * ROW
XSLOTS = 8
BANK = 512
STATROWS = 64
MACROS = R // STATROWS
PER_MACRO = STATROWS // CHUNK
FILLS = C // 4
GK = KW // 4
AFILLS = C // 4
UNITS = R // HALF
OSLOTS = 4
ROOT_AT, SPECTRUM_AT = 7, (11, 12, 13, 15)

T_FW, T_GH, T_EH, T_EW, T_ID, T_MASK = 0, 128, 640, 1152, 1408, 1536
T_ALL = 1568

E_SCALE, H_SCALE = 2.0 ** 20, 2.0 ** 8
TINY = 2.0 ** -60
POWER_BITS = 0x7F800000


def constant_table():
    t = np.zeros((P, T_ALL))
    w = 2 * np.arange(P)[:, None] + np.arange(2)[None, :]
    kw = np.arange(KW)
    a = 2 * np.pi * w[:, :, None] * kw / R
    t[:, T_FW:T_GH] = (np.stack([np.cos(a), -np.sin(a)], 2) / R).reshape(P, -1)
    kh = np.concatenate([np.arange(MODE), np.arange(R - MODE, R)])
    q = np.arange(P)
    h = (q // HALF)[:, None] * CHUNK + np.arange(2)[None, :] * HALF + (q % HALF)[:, None]
    b = 2 * np.pi * ((h[:, :, None] * kh) % R) / R
    g = np.stack([np.stack([np.cos(b), -np.sin(b)], 2), np.stack([np.sin(b), np.cos(b)], 2)], 2)
    t[:, T_GH:T_EH] = g.reshape(P, -1)
    d = 2 * np.pi * ((kh[:, None] * np.arange(R)) % R) / R
    e = np.stack([np.stack([np.cos(d), np.sin(d)], 1), np.stack([-np.sin(d), np.cos(d)], 1)], 0)
    t[:, T_EH:T_EW] = e.reshape(P, -1)
    order = np.array([GK * tt + gk for gk in range(GK) for tt in range(4)])
    f = 2 * np.pi * order[:, None, None] * w.T[None] / R
    s = np.where(order == 0, 1.0, 2.0)[:, None, None] / R
    ew = np.concatenate([s * np.cos(f), -s * np.sin(f)] * 2, 0)
    t[:, T_EW:T_ID] = E_SCALE * ew.reshape(P, -1)
    t[:, T_ID:T_MASK] = np.eye(P)
    t[:, T_MASK:] = (q[:, None] % C) // (C // GROUPS) == np.arange(GROUPS)
    return t.astype(np.float32)


def spectral_layer(nc, x, w0, w1, res_w, res_b, table, out):
    fp32, fp16, int32 = mybir.dt.float32, mybir.dt.float16, mybir.dt.int32
    ALU = mybir.AluOpType
    ACT = mybir.ActivationFunctionType
    AX = mybir.AxisListType
    ds = bass.ds

    x_rows = x.rearrange("n h (p two) c -> p (n h) (two c)", two=2)
    out_rows = out.rearrange("n h (p two) c -> p (n h) (two c)", two=2)
    w0_rows = w0.rearrange("x (q two) i o r -> (two i) x q (o r)", two=2)
    w1_rows = w1.rearrange("x (q two) i o r -> (two i) x q (o r)", two=2)
    mixed = nc.dram_tensor("mixed_modes", [KH, P, 4 * C], fp32).ap()
    mixed_in = mixed.rearrange("k p f -> p k f")
    peaks_dram = nc.dram_tensor("peaks", [P, 1], fp32).ap()
    mixed_out = mixed.rearrange("k (g n r) f -> n r k g f", g=GK, n=N)

    with ExitStack() as ctx:
        def sb(name, shape, dtype=fp32):
            return ctx.enter_context(nc.sbuf_tensor(name, shape, dtype))

        def sem(name):
            return ctx.enter_context(nc.semaphore(name))

        ring = sb("ring", [P, XSLOTS, CELL])
        work = sb("work", [P, 2, C * P])
        spectrum = sb("spectrum", [P, KH, KP, N, 2])
        const = sb("const", [P, T_ALL])
        ones = sb("ones", [P, P])
        w_block = sb("w_block", [P, P])
        w_scaled = sb("w_scaled", [P, P])
        cells = sb("cells", [P, MACROS, GROUPS, 6])
        early = sb("early", [P, GROUPS, 6])
        spread = sb("spread", [P, MACROS, GROUPS, 2])
        sums = sb("sums", [P, GROUPS])
        mean = sb("mean", [P, GROUPS])
        rstd = sb("rstd", [P, GROUPS])
        var = sb("var", [P, GROUPS])
        root = sb("root", [P, GROUPS])
        picked = sb("picked", [P, GROUPS])
        chan = sb("chan", [P, 4])
        scale_all = sb("scale_all", [P, N])
        shift_all = sb("shift_all", [P, N])
        dc_all = sb("dc_all", [P, N])
        ew = sb("ew", [P, 2, 2, P], fp16)
        bias = sb("bias", [1, 2 * C])
        span = sb("span", [P, 8])
        spare = sb("spare", [P, 10])

        psum = ctx.enter_context(nc.psum_tensor("psum", [P, 8, BANK], fp32))

        fw = const[:, T_FW:T_GH].rearrange("p (two m) -> p two m", two=2)
        gh = const[:, T_GH:T_EH].rearrange("p (a r m) -> p a r m", a=2, r=2)
        eh = const[:, T_EH:T_EW].rearrange("p (r h) -> p r h", r=2)
        ew_full = const[:, T_EW:T_ID].rearrange("p (two m) -> p two m", two=2)
        ident = const[:, T_ID:T_MASK]
        mask = const[:, T_MASK:T_ALL]

        x_slot = [ring[:, s, :].rearrange("p (h f) -> p h f", f=ROW) for s in range(XSLOTS)]
        w_slot = [ring[:, s, :].rearrange("p (q o r) -> p q o r", q=KP, r=2) for s in range(XSLOTS)]
        rows_w = work[:, 0, :].rearrange("p (c h) -> p c h", c=C)
        rows_h = work[:, 1, :].rearrange("p (m c) -> p m c", c=C)
        blocks = work[:, 0, 0:4 * KP * 2 * 2 * N * 2].rearrange(
            "p (b q v k n r) -> p b q v k n r", b=4, q=KP, v=2, k=2, n=N)
        mix_out = work[:, 1, 0:4 * 2 * 4 * C].rearrange("p (m k f) -> p m k f", m=4, k=2)
        o_slot = [work[:, 0, s * CELL:(s + 1) * CELL].rearrange("p (h f) -> p h f", f=ROW) for s in range(OSLOTS)]
        flat = spectrum[:, :, :, :, :].rearrange("p a b c d -> p (a b c d)")
        rows_back = flat[:, 0:R * C // 2].bitcast(fp16).rearrange("p (h o) -> p h o", o=C)
        at = R * C // 2
        modes = flat[:, at:at + KW * C].rearrange("p (k o) -> p k o", o=C)
        at += KW * C
        xt = [flat[:, at + b * 2 * BANK:at + (b + 1) * 2 * BANK] for b in range(2)]
        at += 4 * BANK
        peaks = flat[:, at:at + P]
        correction = flat[0:1, at + P:at + P + N * C].rearrange("p (n o) -> p n o", o=C)
        S_PEAK, S_TOP, S_INV, S_POW, S_H, S_Z, S_UNZ, S_NOW = range(8)

        consts_loaded = sem("consts_loaded")
        w_cleared = sem("w_cleared")
        res_loaded = sem("res_loaded")
        ones_set = sem("ones_set")
        x1_loaded = [sem(f"x1_loaded{s}") for s in range(XSLOTS)]
        fw_done = sem("fw_done")
        rows_w_copied = sem("rows_w_copied")
        turned = sem("turned")
        rows_h_copied = sem("rows_h_copied")
        fh_done = sem("fh_done")
        spectrum_copied = sem("spectrum_copied")
        stats_done = sem("stats_done")
        dve_step = sem("dve_step")
        sums_ready = sem("sums_ready")
        totals_ready = sem("totals_ready")
        totals_read = sem("totals_read")
        var_ready = sem("var_ready")
        root_ready = sem("root_ready")
        chan_ready = sem("chan_ready")
        blocks_cleared = sem("blocks_cleared")
        w_loaded = [sem(f"w_loaded{s}") for s in range(XSLOTS)]
        blocks_ready = sem("blocks_ready")
        mix_done = sem("mix_done")
        mix_banks = sem("mix_banks")
        mixed_stored = [sem(f"mixed_stored{m}") for m in range(4)]
        modes_loaded = sem("modes_loaded")
        shifts_summed = sem("shifts_summed")
        correction_ready = sem("correction_ready")
        peak_ready = sem("peak_ready")
        peak_stored = sem("peak_stored")
        peaks_loaded = sem("peaks_loaded")
        scale_ready = sem("scale_ready")
        weights_ready = sem("weights_ready")
        prep_step = sem("prep_step")
        ih_done = sem("ih_done")
        hi_copied = sem("hi_copied")
        lo_copied = sem("lo_copied")
        x2_loaded = [sem(f"x2_loaded{s}") for s in range(OSLOTS)]
        xt_done = sem("xt_done")
        xt_banks = sem("xt_banks")
        z_done = sem("z_done")
        z_banks = sem("z_banks")
        added = sem("added")
        stored = [sem(f"stored{s}") for s in range(OSLOTS)]

        block = ctx.enter_context(nc.Block())

        @block.sync
        def _(sp):
            sp.dma_start(const[:, :], table).then_inc(consts_loaded, 16)
            def load_x(s, row, loaded):
                for part in range(2):
                    sp.dma_start(x_slot[s][:, HALF * part:HALF * (part + 1), :],
                                 x_rows[:, ds(row + HALF * part, HALF), :]).then_inc(loaded[s], 16)

            for s in range(XSLOTS):
                load_x(s, s * CHUNK, x1_loaded)
            for s in range(4):
                sp.dma_start(spare[0:1, s:s + 1], table[0:1, 0:1]).then_inc(stored[s], 16)
                sp.dma_start(spare[0:1, 4 + s:5 + s], table[0:1, 0:1]).then_inc(mixed_stored[s], 16)
            sp.wait_ge(w_cleared, 1)
            for b in range(2):
                sp.dma_start(w_block[b * C:(b + 1) * C, b * C:(b + 1) * C], res_w).then_inc(res_loaded, 16)
            sp.dma_start(bias[0:1, 0:C], res_b.rearrange("(a o) -> a o", a=1)).then_inc(res_loaded, 16)

            def refill(n, macro):
                chunks = sp.snap(CHUNKS * n + PER_MACRO * (macro + 1))
                sp.wait_ge(stats_done, chunks)
                sp.wait_ge(fw_done, chunks)
                for j in range(PER_MACRO):
                    s = (macro % 2) * PER_MACRO + j
                    load_x(s, R * n + STATROWS * (macro + 2) + CHUNK * j, x1_loaded)

            with sp.Fori(0, N - 1) as n:
                for macro in range(MACROS):
                    refill(n, macro)
            for macro in range(MACROS - 2):
                refill(N - 1, macro)

            def load_weights(s, it):
                rows = w0_rows if s < 4 else w1_rows
                for part in range(2):
                    sp.dma_start(ring[:, s, part * CELL // 2:(part + 1) * CELL // 2].rearrange(
                                     "p (a q f) -> p a q f", a=1, f=2 * C),
                                 rows[:, ds(4 * it + s % 4, 1), part * KP // 2:(part + 1) * KP // 2, :]
                                 ).then_inc(w_loaded[s], 16)

            for macro in range(2):
                sp.wait_ge(stats_done, CHUNKS * (N - 1) + PER_MACRO * (MACROS - 1 + macro))
                sp.wait_ge(fw_done, CHUNKS * (N - 1) + PER_MACRO * (MACROS - 1 + macro))
                for s in range(4 * macro, 4 * macro + 4):
                    load_weights(s, 0)
            with sp.Fori(0, 7) as it:
                for s in range(XSLOTS):
                    sp.wait_ge(mix_done, 4 + 8 * it + s + 1)
                    load_weights(s, it + 1)

            for s in range(OSLOTS):
                sp.wait_ge(mix_done, 4 + KH - 8 + s + 1)
                load_x(s, s * CHUNK, x2_loaded)
            with sp.Fori(0, N * CHUNKS // OSLOTS - 1) as four:
                for s in range(OSLOTS):
                    sp.wait_ge(added, OSLOTS * four + s + 1)
                    load_x(s, CHUNK * (OSLOTS * four + s + OSLOTS), x2_loaded)
                    sp.dma_start(out_rows[:, ds(CHUNK * (OSLOTS * four + s), CHUNK), :], o_slot[s]
                                 ).then_inc(stored[s], 16)
            last = N * CHUNKS - OSLOTS
            for s in range(OSLOTS):
                sp.wait_ge(added, last + s + 1)
                sp.dma_start(out_rows[:, CHUNK * (last + s):CHUNK * (last + s + 1), :], o_slot[s]
                             ).then_inc(stored[s], 16)
            for s in range(OSLOTS):
                sp.wait_ge(stored[s], 16 * (N * CHUNKS // OSLOTS + 1))

        @block.gpsimd
        def _(pool):
            pool.memset(w_block[:, :], 0.0).then_inc(w_cleared, 1)
            pool.memset(ones[:, :], 1.0).then_inc(ones_set, 1)
            for m in range(4):
                pool.wait_ge(mixed_stored[m], 16 * 9)

            def load_modes(n):
                for ri in range(2):
                    pool.dma_start(modes[ri * KH:(ri + 1) * KH].rearrange("p (g t) o -> p g (t o)", t=4),
                                   mixed_out[n, ri]).then_inc(modes_loaded, 16)

            load_modes(0)
            with pool.Fori(0, N - 1) as n:
                pool.wait_ge(ih_done, AFILLS * (n + 1))
                load_modes(n + 1)

        @block.scalar
        def _(act):
            act.wait_ge(consts_loaded, 16)
            nc.scalar.copy(spare[:, 8:9], const[:, 0:1]).then_inc(mix_banks, 4)
            nc.scalar.copy(spare[:, 9:10], const[:, 0:1]).then_inc(z_banks, 2)

            def copy_rows_w(n, k):
                act.wait_ge(fw_done, CHUNKS * n + k + 1)
                nc.scalar.copy(rows_w[:, :, HALF * k:HALF * (k + 1)],
                               psum[:, k % 2, :].rearrange("p (h c) -> p c h", c=C)).then_inc(rows_w_copied, 1)

            def copy_rows_h(n):
                for f in range(FILLS):
                    act.wait_ge(turned, FILLS * n + f + 1)
                    nc.scalar.copy(rows_h[:, :, 4 * f:4 * f + 4],
                                   psum[:, 2 + f % 2, :].rearrange("p (c m) -> p m c", c=4)).then_inc(rows_h_copied, 1)

            def take_root(n):
                act.wait_ge(var_ready, n + 1)
                nc.scalar.activation(root[:, :], var[:, :], ACT.Sqrt).then_inc(root_ready, 1)

            def copy_spectrum(n, b):
                act.wait_ge(fh_done, 4 * n + b + 1)
                act.wait_ge(chan_ready, n + 1)
                nc.scalar.activation(spectrum[:, :, 4 * b:4 * b + 4, ds(n, 1), :].rearrange("p k q n r -> p q (n r) k"),
                                     psum[:, 4 + b, :].rearrange("p (q r k) -> p q r k", q=4, r=2),
                                     ACT.Identity, scale=chan[:, 0:1]).then_inc(spectrum_copied, 1)

            for k in range(CHUNKS):
                copy_rows_w(0, k)
            copy_rows_h(0)
            with act.Fori(0, N - 1) as n:
                for k in range(CHUNKS):
                    copy_rows_w(n + 1, k)
                    if k == ROOT_AT:
                        take_root(n)
                    if k in SPECTRUM_AT:
                        copy_spectrum(n, SPECTRUM_AT.index(k))
                copy_rows_h(n + 1)
            take_root(N - 1)
            for b in range(4):
                copy_spectrum(N - 1, b)

            def mix_copy(it, m):
                act.wait_ge(mix_done, 4 + 8 * it + 2 * m + 2)
                act.wait_ge(mixed_stored[m], 16 * (it + 1))
                nc.scalar.copy(mix_out[:, m, :, :], psum[:, m, :].rearrange("p (k f) -> p k f", k=2)
                               ).then_inc(mix_banks, 1)
                act.wait_ge(mix_banks, 4 + 4 * it + m + 1)
                kh = 4 * it + 2 * m if m < 2 else 4 * it + MODE + 2 * (m - 2)
                act.dma_start(mixed_in[:, ds(kh, 2), :], mix_out[:, m, :, :]).then_inc(mixed_stored[m], 16)

            with act.Fori(0, 8) as it:
                for m in range(4):
                    mix_copy(it, m)

            def silu(n, it, v):
                unit = UNITS * n + 8 * it + v
                s = v // 2
                if v % 2 == 0:
                    act.wait_ge(stored[s], 16 * (4 * n + it + 1))
                act.wait_ge(z_done, unit + 1)
                bank = 2 * (v % 2)
                nc.scalar.activation(
                    o_slot[s][:, HALF * (v % 2):HALF * (v % 2 + 1), :],
                    psum[:, bank:bank + 2, :].rearrange("p b (h f) -> p (b h) f", f=ROW),
                    ACT.Silu, scale=span[:, S_NOW:S_NOW + 1]).then_inc(z_banks, 1)

            def copy_hi(n):
                for f in range(AFILLS):
                    act.wait_ge(ih_done, AFILLS * n + f + 1)
                    for half in range(2):
                        rows = slice(C * half, C * (half + 1))
                        o = 32 * half + 2 * f
                        ins = nc.scalar.activation(rows_back[rows, :, o:o + 2],
                                                   psum[rows, f % 4, :].rearrange("p (o h) -> p h o", o=2),
                                                   ACT.Identity, scale=span[rows, S_H:S_H + 1])
                    ins.then_inc(hi_copied, 1)

            def store_peak(n):
                act.wait_ge(peak_ready, n + 1)
                act.dma_start(peaks_dram, span[:, S_PEAK:S_PEAK + 1]).then_inc(peak_stored, 16)

            def load_peaks(n):
                act.wait_ge(peak_stored, 16 * (n + 1))
                act.dma_start(peaks, peaks_dram.rearrange("p a -> (p a)").partition_broadcast(P)
                              ).then_inc(peaks_loaded, 16)

            def silus(n, it, ahead=False):
                for v in range(8):
                    silu(n, it, v)
                    if ahead and v == 2:
                        store_peak(n + 1)
                    if ahead and v == 3:
                        load_peaks(n + 1)

            def begin(n):
                act.wait_ge(scale_ready, n + 1)
                copy_hi(n)
                act.wait_ge(weights_ready, n + 1)

            store_peak(0)
            load_peaks(0)
            begin(0)
            with act.Fori(0, N - 1) as n:
                with act.Fori(0, 3) as it:
                    silus(n, it)
                silus(n, 3, ahead=True)
                begin(n + 1)
            with act.Fori(0, 4) as it:
                silus(N - 1, it)

        @block.vector
        def _(dve):
            dve.wait_ge(consts_loaded, 16)
            nc.vector.tensor_copy(ew[:, 0, :, :], ew_full).then_inc(prep_step, 1)
            dve.wait_ge(prep_step, 1)
            nc.vector.tensor_tensor(ew[:, 1, :, :], ew_full, ew[:, 0, :, :], ALU.subtract).then_inc(prep_step, 1)

            steps = [0]
            STEPS = 14

            def step(n, ins):
                steps[0] += 1
                ins.then_inc(dve_step, 1)
                dve.wait_ge(dve_step, STEPS * n + steps[0])

            means = cells[:, :, :, 1:5:3]
            moments = cells[:, :, :, 2:6:3]

            def measure(n, macro, target):
                for j in range(PER_MACRO):
                    dve.wait_ge(x1_loaded[(macro % 2) * PER_MACRO + j], 32 * (2 * n + macro // 2 + 1))
                s = (macro % 2) * PER_MACRO
                rows = ring[:, s:s + PER_MACRO, :].rearrange("p s (h two c) -> p (s h) two c", two=2, c=C)
                for g in range(GROUPS):
                    ins = nc.vector.bn_stats(target[:, g, :], rows[:, :, :, 2 * g:2 * g + 2])
                ins.then_inc(stats_done, PER_MACRO)

            def sum_means(n):
                dve.wait_ge(stats_done, CHUNKS * (n + 1))
                nc.vector.tensor_reduce(sums[:, :], means.rearrange("p m g s -> p g m s"), AX.XY, ALU.add
                                        ).then_inc(sums_ready, 1)

            def sum_squares(n):
                steps[0] = 0
                dve.wait_ge(totals_ready, 2 * n + 1)
                step(n, nc.vector.tensor_scalar(mean[:, :], psum[:, 2, 0:GROUPS],
                                                1.0 / (P * MACROS * 2), None, ALU.mult))
                step(n, nc.vector.tensor_tensor(
                    spread[:, :, :, :], means,
                    mean[:, :].rearrange("p (a g b) -> p a g b", a=1, b=1).to_broadcast([P, MACROS, GROUPS, 2]),
                    ALU.subtract))
                step(n, nc.vector.tensor_tensor(spread[:, :, :, :], spread[:, :, :, :], spread[:, :, :, :], ALU.mult))
                step(n, nc.vector.scalar_tensor_tensor(spread[:, :, :, :], spread[:, :, :, :],
                                                       float(STATROWS * 2), moments, ALU.mult, ALU.add))
                nc.vector.tensor_reduce(sums[:, :], spread[:, :, :, :].rearrange("p m g s -> p g m s"), AX.XY, ALU.add
                                        ).then_inc(sums_ready, 1)

            def find_var(n):
                dve.wait_ge(totals_ready, 2 * n + 2)
                nc.vector.tensor_scalar(var[:, :], psum[:, 3, 0:GROUPS], 1.0 / (R * R * (C // GROUPS)), EPS,
                                        ALU.mult, ALU.add).then_inc(var_ready, 1)

            def find_scale_of_image(n):
                dve.wait_ge(root_ready, n + 1)
                step(n, nc.vector.reciprocal(rstd[:, :], root[:, :]))
                step(n, nc.vector.tensor_tensor(root[:, :], rstd[:, :], rstd[:, :], ALU.mult))
                step(n, nc.vector.tensor_tensor(root[:, :], root[:, :], var[:, :], ALU.mult))
                step(n, nc.vector.tensor_scalar(root[:, :], root[:, :], -0.5, 1.5, ALU.mult, ALU.add))
                step(n, nc.vector.tensor_tensor(rstd[:, :], rstd[:, :], root[:, :], ALU.mult))
                step(n, nc.vector.tensor_tensor(picked[:, :], rstd[:, :], mask, ALU.mult))
                step(n, nc.vector.tensor_reduce(chan[:, 0:1], picked[:, :], AX.X, ALU.add))
                step(n, nc.vector.tensor_tensor(picked[:, :], mean[:, :], mask, ALU.mult))
                step(n, nc.vector.tensor_reduce(chan[:, 1:2], picked[:, :], AX.X, ALU.add))
                step(n, nc.vector.tensor_tensor(chan[:, 2:3], chan[:, 0:1], chan[:, 1:2], ALU.mult))
                nc.vector.tensor_scalar(scale_all[:, ds(n, 1)], chan[:, 0:1], 1.0, None, ALU.mult)
                nc.vector.tensor_scalar(shift_all[:, ds(n, 1)], chan[:, 2:3], 1.0, None, ALU.mult)
                nc.vector.tensor_scalar(dc_all[:, ds(n, 1)], chan[:, 2:3], -float(R), None, ALU.mult
                                        ).then_inc(chan_ready, 1)
                assert steps[0] == STEPS

            for macro in range(MACROS):
                measure(0, macro, cells[:, macro])
            with dve.Fori(0, N - 1) as n:
                sum_means(n)
                measure(n + 1, 0, early)
                sum_squares(n)
                dve.wait_ge(stats_done, CHUNKS * (n + 1) + PER_MACRO)
                nc.vector.tensor_scalar(cells[:, 0, :, :], early[:, :, :], 1.0, None, ALU.mult)
                measure(n + 1, 1, cells[:, 1])
                find_var(n)
                measure(n + 1, 2, cells[:, 2])
                find_scale_of_image(n)
                measure(n + 1, 3, cells[:, 3])
            sum_means(N - 1)
            sum_squares(N - 1)
            find_var(N - 1)
            find_scale_of_image(N - 1)

            dve.wait_ge(fh_done, 4 * N)
            dve.wait_ge(rows_h_copied, FILLS * N)
            nc.vector.memset(blocks.rearrange("p b q v k n r -> p (b q v k n r)"), 0.0).then_inc(blocks_cleared, 1)
            dve.wait_ge(spectrum_copied, 4 * N)
            nc.vector.tensor_tensor(spectrum[0:C, 0, 0, :, 0], spectrum[0:C, 0, 0, :, 0], dc_all[0:C, :], ALU.add
                                    ).then_inc(blocks_cleared, 1)
            dve.wait_ge(blocks_cleared, 2)
            with dve.Fori(0, 8) as it:
                for s in range(8):
                    dve.wait_ge(mix_done, 8 * it + s + 1)
                    kh = 4 * it + s if s < 4 else 4 * it + MODE + s - 4
                    for half in range(2):
                        rows = slice(C * half, C * (half + 1))
                        z = spectrum[rows, kh, :, :, :]
                        b = blocks[rows, s % 4, :, :, half, :, :]
                        nc.vector.tensor_scalar(b[:, :, 0], z, 1.0, None, ALU.mult)
                        nc.vector.tensor_scalar(b[:, :, 1, :, 0], z[:, :, :, 1], -1.0, None, ALU.mult)
                        ins = nc.vector.tensor_scalar(b[:, :, 1, :, 1], z[:, :, :, 0], 1.0, None, ALU.mult)
                    ins.then_inc(blocks_ready, 1)

            def xt_copy(n, it, v):
                dve.wait_ge(xt_done, UNITS * n + 8 * it + v + 1)
                nc.vector.tensor_copy(xt[v % 2].rearrange("p (b f) -> p b f", b=2),
                                      psum[:, 4 + 2 * (v % 2):6 + 2 * (v % 2), :]).then_inc(xt_banks, 1)

            def add_x(n, it, v):
                dve.wait_ge(z_banks, UNITS * n + 8 * it + v + 3)
                rows = slice(HALF * (v % 2), HALF * (v % 2 + 1))
                s = v // 2
                ins = nc.vector.tensor_tensor(o_slot[s][:, rows, :], o_slot[s][:, rows, :], x_slot[s][:, rows, :],
                                              ALU.add)
                if v % 2:
                    ins.then_inc(added, 1)

            def units(n, it, last=False, ahead=False):
                for v in range(8):
                    if not (last and v == 7):
                        xt_copy(n, it, v + 1) if v < 7 else xt_copy(n, it + 1, 0)
                    if ahead and v == 1:
                        find_peak(n + 1)
                    if ahead and v == 5:
                        find_scale(n + 1)
                    add_x(n, it, v)

            PREP = 8
            prepared = [0]

            def prep(n, ins):
                prepared[0] += 1
                ins.then_inc(prep_step, 1)
                dve.wait_ge(prep_step, 2 + PREP * n + prepared[0])

            def col(k):
                return span[:, k:k + 1]

            def find_peak(n):
                prepared[0] = 0
                prep(n, nc.vector.tensor_scalar(bias[0:1, C:2 * C].rearrange("p (a o) -> p a o", a=1),
                                                correction[:, ds(n, 1), :], 1.0, None, ALU.mult))
                dve.wait_ge(modes_loaded, 32 * (n + 1))
                prep(n, nc.vector.tensor_tensor(modes[0:1, 0, :], modes[0:1, 0, :], bias[0:1, C:2 * C], ALU.add))
                nc.vector.tensor_reduce(col(S_PEAK), modes.rearrange("p k o -> p (k o)"), AX.X, ALU.max,
                                        apply_absolute_value=True).then_inc(peak_ready, 1)

            def find_scale(n):
                dve.wait_ge(peaks_loaded, 16 * (n + 1))
                prep(n, nc.vector.tensor_reduce(col(S_TOP), peaks, AX.X, ALU.max))
                prep(n, nc.vector.tensor_scalar(col(S_TOP), col(S_TOP), TINY, None, ALU.max))
                prep(n, nc.vector.reciprocal(col(S_INV), col(S_TOP)))
                prep(n, nc.vector.tensor_scalar(col(S_POW).bitcast(int32), col(S_INV).bitcast(int32), POWER_BITS, None,
                                                ALU.bitwise_and))
                prep(n, nc.vector.tensor_scalar(col(S_Z), col(S_POW), H_SCALE * E_SCALE, None, ALU.mult))
                prep(n, nc.vector.reciprocal(col(S_UNZ), col(S_Z)))
                nc.vector.tensor_scalar(col(S_H), col(S_POW), H_SCALE, None, ALU.mult).then_inc(scale_ready, 1)
                assert prepared[0] == PREP

            def begin(n):
                xt_copy(n, 0, 0)
                nc.vector.tensor_scalar(col(S_NOW), col(S_UNZ), 1.0, None, ALU.mult)
                nc.vector.tensor_scalar(chan[:, 0:1], scale_all[:, ds(n, 1)], 1.0, None, ALU.mult
                                        ).then_inc(dve_step, 1)
                dve.wait_ge(dve_step, STEPS * N + 2 * n + 1)
                nc.vector.tensor_scalar(chan[:, 1:2], chan[:, 0:1], col(S_Z), None, ALU.mult).then_inc(dve_step, 1)
                dve.wait_ge(dve_step, STEPS * N + 2 * n + 2)
                nc.vector.tensor_scalar(w_scaled[:, :], w_block[:, :], chan[:, 1:2], None, ALU.mult
                                        ).then_inc(weights_ready, 1)
                dve.wait_ge(scale_ready, n + 1)
                for f in range(AFILLS):
                    dve.wait_ge(hi_copied, AFILLS * n + f + 1)
                    for half in range(2):
                        rows = slice(C * half, C * (half + 1))
                        other = slice(C * (1 - half), C * (2 - half))
                        o = 32 * half + 2 * f
                        ins = nc.vector.scalar_tensor_tensor(
                            rows_back[other, :, o:o + 2], psum[rows, f % 4, :].rearrange("p (o h) -> p h o", o=2),
                            span[rows, S_H:S_H + 1], rows_back[rows, :, o:o + 2], ALU.mult, ALU.subtract)
                    ins.then_inc(lo_copied, 1)

            dve.wait_ge(res_loaded, 48)
            nc.vector.tensor_scalar(bias[0:1, 0:C], bias[0:1, 0:C], float(R), None, ALU.mult).then_inc(xt_banks, 2)
            dve.wait_ge(xt_banks, 2)
            dve.wait_ge(shifts_summed, N)
            nc.vector.scalar_tensor_tensor(
                correction, psum[0:1, 4, :].rearrange("p (n o) -> p n o", o=C), -float(R),
                bias[0:1, 0:C].rearrange("p (a o) -> p a o", a=1).to_broadcast([1, N, C]), ALU.mult, ALU.add
            ).then_inc(correction_ready, 1)
            dve.wait_ge(correction_ready, 1)
            find_peak(0)
            find_scale(0)
            begin(0)
            with dve.Fori(0, N - 1) as n:
                with dve.Fori(0, 3) as it:
                    units(n, it)
                units(n, 3, last=True, ahead=True)
                begin(n + 1)
            with dve.Fori(0, 3) as it:
                units(N - 1, it)
            units(N - 1, 3, last=True)

        @block.tensor
        def _(pe):
            pe.wait_ge(consts_loaded, 16)
            pe.wait_ge(ones_set, 1)
            nc.tensor.matmul(psum[:, 0, 0:P], ones[:, :], ones[:, :], start=True, stop=True).then_inc(mix_done, 4)

            def total(n, which):
                pe.wait_ge(sums_ready, 2 * n + which + 1)
                nc.tensor.matmul(psum[:, 2 + which, 0:GROUPS], ones[:, :], sums[:, :], start=True, stop=True
                                 ).then_inc(totals_ready, 1)

            def along_w(n, k):
                if k >= 2:
                    pe.wait_ge(rows_w_copied, CHUNKS * n + k - 1)
                pe.wait_ge(x1_loaded[k % XSLOTS], 32 * (2 * n + k // XSLOTS + 1))
                for two in range(2):
                    for half in range(2):
                        ins = nc.tensor.matmul(
                            psum[half * C:(half + 1) * C, k % 2, :], fw[:, two, :],
                            x_slot[k % XSLOTS][:, HALF * half:HALF * (half + 1), two * C:(two + 1) * C],
                            start=two == 0, stop=two == 1)
                ins.then_inc(fw_done, 1)

            def turn(n):
                pe.wait_ge(rows_w_copied, CHUNKS * (n + 1))
                for f in range(FILLS):
                    if f >= 2:
                        pe.wait_ge(rows_h_copied, FILLS * n + f - 1)
                    for c in range(4):
                        ins = nc.tensor.transpose(psum[:, 2 + f % 2, c * P:(c + 1) * P], rows_w[:, 4 * f + c, :], ident)
                    ins.then_inc(turned, 1)

            def along_h(n, q):
                if q == 0:
                    pe.wait_ge(rows_h_copied, FILLS * (n + 1))
                for half in range(2):
                    for ri in range(2):
                        for odd in range(2):
                            m = half * 2 * KW + ri * KW + 2 * q + odd
                            ins = nc.tensor.matmul(psum[odd * C:(odd + 1) * C, 4 + q // 4, (q % 4) * P:(q % 4 + 1) * P],
                                                   rows_h[:, m, :], gh[:, half, ri, :],
                                                   start=(half, ri) == (0, 0), stop=(half, ri) == (1, 1))
                if q % 4 == 3:
                    ins.then_inc(fh_done, 1)
                if q in (1, 2):
                    total(n, q - 1)

            for k in range(CHUNKS):
                along_w(0, k)
            turn(0)
            with pe.Fori(0, N - 1) as n:
                for k in range(CHUNKS):
                    along_w(n + 1, k)
                    along_h(n, k)
                pe.wait_ge(chan_ready, n + 1)
                turn(n + 1)
            for q in range(KP):
                along_h(N - 1, q)

            pe.wait_ge(chan_ready, N)
            pe.wait_ge(spectrum_copied, 4 * N)
            pe.wait_ge(res_loaded, 48)
            for n in range(N):
                nc.tensor.matmul(psum[0:1, 4, n * C:(n + 1) * C], shift_all[:, n:n + 1], w_block[:, 0:C],
                                 start=True, stop=True).then_inc(shifts_summed, 1)

            with pe.Fori(0, 8) as it:
                for s in range(8):
                    pe.wait_ge(blocks_ready, 8 * it + s + 1)
                    pe.wait_ge(w_loaded[s], 32 * (it + 1))
                    if s % 2 == 0:
                        pe.wait_ge(mix_banks, 4 * it + s // 2 + 1)
                    for t in range(4):
                        for v in range(2):
                            for g in range(4):
                                ins = nc.tensor.matmul(
                                    psum[32 * g:32 * (g + 1), s // 2, (4 * (s % 2) + t) * C:(4 * (s % 2) + t + 1) * C],
                                    blocks[:, s % 4, 4 * t + g, v, :, :, :].rearrange("p k n r -> p (k n r)"), w_slot[s][:, 4 * t + g, :, v],
                                    start=v == 0, stop=v == 1)
                    ins.then_inc(mix_done, 1)

            def transpose_x(n, it, v):
                s = v // 2
                if v % 2 == 0:
                    pe.wait_ge(x2_loaded[s], 32 * (4 * n + it + 1))
                pe.wait_ge(xt_banks, UNITS * n + 8 * it + v + 1)
                for row in range(HALF):
                    ins = nc.tensor.transpose(psum[:, 4 + 2 * (v % 2) + row // 4, (row % 4) * P:(row % 4 + 1) * P],
                                              x_slot[s][:, HALF * (v % 2) + row, :], ident)
                ins.then_inc(xt_done, 1)

            def sum_unit(n, it, v):
                pe.wait_ge(xt_banks, UNITS * n + 8 * it + v + 3)
                pe.wait_ge(z_banks, UNITS * n + 8 * it + v + 1)
                if v == 0:
                    pe.wait_ge(weights_ready, n + 1)
                    pe.wait_ge(hi_copied, AFILLS * (n + 1))
                    pe.wait_ge(lo_copied, AFILLS * (n + 1))
                for four in range(2):
                    row = HALF * (8 * it + v) + 4 * four
                    z = psum[:, 2 * (v % 2) + four, :].rearrange("p (h two o) -> p h two o", two=2, o=C)
                    for two in range(2):
                        for part in range(2):
                            nc.tensor.matmul(z[:, :, two, :], ew[:, part, two, :], rows_back[:, ds(row, 4), :],
                                             start=(two, part) == (0, 0), stop=False, skip_group_check=True)
                    for h in range(4):
                        c0 = (4 * four + h) * P
                        ins = nc.tensor.matmul(z[:, h, :, :], xt[v % 2][:, c0:c0 + P], w_scaled[:, :],
                                               start=False, stop=h == 3, skip_group_check=True)
                ins.then_inc(z_done, 1)

            def units(n, it, last):
                for v in range(8):
                    if not (last and v == 7):
                        transpose_x(n, it, v + 1) if v < 7 else transpose_x(n, it + 1, 0)
                    sum_unit(n, it, v)

            pe.wait_ge(mix_banks, 4 + 4 * 8)
            pe.wait_ge(correction_ready, 1)
            pe.wait_ge(prep_step, 2)
            with pe.Fori(0, N) as n:
                transpose_x(n, 0, 0)
                pe.wait_ge(peak_ready, n + 1)
                pe.wait_ge(z_banks, UNITS * n + 2)
                for f in range(AFILLS):
                    if f >= 4:
                        pe.wait_ge(hi_copied, AFILLS * n + f - 3)
                        pe.wait_ge(lo_copied, AFILLS * n + f - 3)
                    for o in range(2):
                        for half in range(2):
                            for ri in range(2):
                                tile = 2 * half + ri
                                ins = nc.tensor.matmul(psum[32 * tile:32 * (tile + 1), f % 4, o * R:(o + 1) * R],
                                                       modes[:, :, 32 * half + 2 * f + o], eh[:, ri, :],
                                                       start=True, stop=True)
                    ins.then_inc(ih_done, 1)
                with pe.Fori(0, 3) as it:
                    units(n, it, False)
                units(n, 3, True)


def kernel(x, L0_conv_w0, L0_conv_w1, L0_conv_res_w, L0_conv_res_b):
    import concourse.bacc as bacc
    from concourse.bass_utils import run_bass_kernel_spmd

    nc = bacc.Bacc("TRN2", target_bir_lowering=False, num_devices=1)
    arrays, args = {}, []
    for name, a in (("x", x), ("w0", L0_conv_w0), ("w1", L0_conv_w1), ("res_w", L0_conv_res_w),
                    ("res_b", L0_conv_res_b), ("table", constant_table())):
        a = np.ascontiguousarray(a)
        arrays[name] = a
        args.append(nc.dram_tensor(name, a.shape, mybir.dt.from_np(a.dtype), kind="ExternalInput").ap())
    out = nc.dram_tensor("out", (N, R, R, C), mybir.dt.float32, kind="ExternalOutput").ap()
    spectral_layer(nc, *args, out)
    return run_bass_kernel_spmd(nc, [arrays], core_ids=[0]).results[0]["out"]
```

```python
from contextlib import ExitStack

import numpy as np
import concourse.bass as bass
from concourse import mybir

N, R, C, MODE = 8, 256, 64, 32
P = 128
KW, KH = MODE, 2 * MODE
KP = KW // 2
GROUPS, EPS = 32, 1e-5
CHUNK = 16
CHUNKS = R // CHUNK
HALF = CHUNK // 2
ROW = 2 * C
CELL = CHUNK * ROW
XSLOTS = 8
BANK = 512
STATROWS = 64
MACROS = R // STATROWS
PER_MACRO = STATROWS // CHUNK
FILLS = C // 4
GK = KW // 4
AFILLS = C // 4
UNITS = R // HALF
OSLOTS = 4
TURN_BANKS = (0, 1, 2, 3)
FIRST_BANKS = (6, 7, 0, 1, 2, 3)
AHEAD_BANK = 6
AHEAD_AT = (0, 2, 3, 4, 6)
FIRST_AT = 6
ROOT_AT, SPECTRUM_AT = 7, (11, 12, 13, 15)

T_FW, T_GH, T_EH, T_EW, T_ID, T_MASK = 0, 128, 640, 1152, 1408, 1536
T_ALL = 1568

E_SCALE, H_SCALE = 2.0 ** 20, 2.0 ** 8
TINY = 2.0 ** -60
POWER_BITS = 0x7F800000


def constant_table():
    t = np.zeros((P, T_ALL))
    w = 2 * np.arange(P)[:, None] + np.arange(2)[None, :]
    kw = np.arange(KW)
    a = 2 * np.pi * w[:, :, None] * kw / R
    t[:, T_FW:T_GH] = (np.stack([np.cos(a), -np.sin(a)], 2) / R).reshape(P, -1)
    kh = np.concatenate([np.arange(MODE), np.arange(R - MODE, R)])
    q = np.arange(P)
    h = (q // HALF)[:, None] * CHUNK + np.arange(2)[None, :] * HALF + (q % HALF)[:, None]
    b = 2 * np.pi * ((h[:, :, None] * kh) % R) / R
    g = np.stack([np.stack([np.cos(b), -np.sin(b)], 2), np.stack([np.sin(b), np.cos(b)], 2)], 2)
    t[:, T_GH:T_EH] = g.reshape(P, -1)
    d = 2 * np.pi * ((kh[:, None] * np.arange(R)) % R) / R
    e = np.stack([np.stack([np.cos(d), np.sin(d)], 1), np.stack([-np.sin(d), np.cos(d)], 1)], 0)
    t[:, T_EH:T_EW] = e.reshape(P, -1)
    order = np.array([GK * tt + gk for gk in range(GK) for tt in range(4)])
    f = 2 * np.pi * order[:, None, None] * w.T[None] / R
    s = np.where(order == 0, 1.0, 2.0)[:, None, None] / R
    ew = np.concatenate([s * np.cos(f), -s * np.sin(f)] * 2, 0)
    t[:, T_EW:T_ID] = E_SCALE * ew.reshape(P, -1)
    t[:, T_ID:T_MASK] = np.eye(P)
    t[:, T_MASK:] = (q[:, None] % C) // (C // GROUPS) == np.arange(GROUPS)
    return t.astype(np.float32)


def spectral_layer(nc, x, w0, w1, res_w, res_b, table, out):
    fp32, fp16, int32 = mybir.dt.float32, mybir.dt.float16, mybir.dt.int32
    ALU = mybir.AluOpType
    ACT = mybir.ActivationFunctionType
    AX = mybir.AxisListType
    ds = bass.ds

    x_rows = x.rearrange("n h (p two) c -> p (n h) (two c)", two=2)
    out_rows = out.rearrange("n h (p two) c -> p (n h) (two c)", two=2)
    w0_rows = w0.rearrange("x (q two) i o r -> (two i) x q (o r)", two=2)
    w1_rows = w1.rearrange("x (q two) i o r -> (two i) x q (o r)", two=2)
    mixed = nc.dram_tensor("mixed_modes", [KH, P, 4 * C], fp32).ap()
    mixed_in = mixed.rearrange("k p f -> p k f")
    peaks_dram = nc.dram_tensor("peaks", [P, 1], fp32).ap()
    mixed_out = mixed.rearrange("k (g n r) f -> n r k g f", g=GK, n=N)

    with ExitStack() as ctx:
        def sb(name, shape, dtype=fp32):
            return ctx.enter_context(nc.sbuf_tensor(name, shape, dtype))

        def sem(name):
            return ctx.enter_context(nc.semaphore(name))

        ring = sb("ring", [P, XSLOTS, CELL])
        work = sb("work", [P, 2, C * P])
        spectrum = sb("spectrum", [P, KH, KP, N, 2])
        const = sb("const", [P, T_ALL])
        ones = sb("ones", [P, P])
        w_block = sb("w_block", [P, P])
        w_scaled = sb("w_scaled", [P, 2, P])
        cells = sb("cells", [P, MACROS, GROUPS, 6])
        early = sb("early", [P, GROUPS, 6])
        spread = sb("spread", [P, MACROS, GROUPS, 2])
        sums = sb("sums", [P, GROUPS])
        mean = sb("mean", [P, GROUPS])
        rstd = sb("rstd", [P, GROUPS])
        var = sb("var", [P, GROUPS])
        root = sb("root", [P, GROUPS])
        picked = sb("picked", [P, GROUPS])
        chan = sb("chan", [P, 4])
        scale_all = sb("scale_all", [P, N])
        shift_all = sb("shift_all", [P, N])
        dc_all = sb("dc_all", [P, N])
        ew = sb("ew", [P, 2, 2, P], fp16)
        bias = sb("bias", [1, C])
        span = sb("span", [P, 12])
        spare = sb("spare", [P, 10])

        psum = ctx.enter_context(nc.psum_tensor("psum", [P, 8, BANK], fp32))

        fw = const[:, T_FW:T_GH].rearrange("p (two m) -> p two m", two=2)
        gh = const[:, T_GH:T_EH].rearrange("p (a r m) -> p a r m", a=2, r=2)
        eh = const[:, T_EH:T_EW].rearrange("p (r h) -> p r h", r=2)
        ew_full = const[:, T_EW:T_ID].rearrange("p (two m) -> p two m", two=2)
        ident = const[:, T_ID:T_MASK]
        mask = const[:, T_MASK:T_ALL]

        x_slot = [ring[:, s, :].rearrange("p (h f) -> p h f", f=ROW) for s in range(XSLOTS)]
        w_slot = [ring[:, s, :].rearrange("p (q o r) -> p q o r", q=KP, r=2) for s in range(XSLOTS)]
        rows_w = work[:, 0, :].rearrange("p (c h) -> p c h", c=C)
        rows_h = work[:, 1, :].rearrange("p (m c) -> p m c", c=C)
        blocks = work[:, 0, 0:4 * KP * 2 * 2 * N * 2].rearrange(
            "p (b q v k n r) -> p b q v k n r", b=4, q=KP, v=2, k=2, n=N)
        mix_out = work[:, 1, 0:4 * 2 * 4 * C].rearrange("p (m k f) -> p m k f", m=4, k=2)
        o_slot = [work[:, 0, s * CELL:(s + 1) * CELL].rearrange("p (h f) -> p h f", f=ROW) for s in range(OSLOTS)]
        flat = spectrum[:, :, :, :, :].rearrange("p a b c d -> p (a b c d)")
        rows_back = [a.bitcast(fp16).rearrange("p (h o) -> p h o", o=C) for a in (
            flat[:, 0:R * C // 2], ring[:, XSLOTS // 2:, :].rearrange("p s f -> p (s f)"))]
        at = R * C // 2
        modes = flat[:, at:at + KW * C].rearrange("p (k o) -> p k o", o=C)
        at += KW * C
        xt = [flat[:, at + b * 2 * BANK:at + (b + 1) * 2 * BANK] for b in range(2)]
        at += 4 * BANK
        peaks = flat[:, at:at + P]
        correction = flat[0:1, at + P:at + P + N * C].rearrange("p (n o) -> p n o", o=C)
        at += P + N * C
        PIECE = len(AHEAD_AT)
        picked_modes = flat[:, at:at + 4 * PIECE * KW].rearrange("p (half o k) -> p half o k", half=2, k=KW)
        S_PEAK, S_TOP, S_INV, S_POW, S_H, S_Z, S_CHAN, S_W, S_HALF, S_UNZ = range(10)

        consts_loaded = sem("consts_loaded")
        w_cleared = sem("w_cleared")
        res_loaded = sem("res_loaded")
        ones_set = sem("ones_set")
        x1_loaded = [sem(f"x1_loaded{s}") for s in range(XSLOTS)]
        fw_done = sem("fw_done")
        rows_w_copied = sem("rows_w_copied")
        turned = sem("turned")
        rows_h_copied = sem("rows_h_copied")
        fh_done = sem("fh_done")
        spectrum_copied = sem("spectrum_copied")
        stats_done = sem("stats_done")
        dve_step = sem("dve_step")
        sums_ready = sem("sums_ready")
        totals_ready = sem("totals_ready")
        var_ready = sem("var_ready")
        root_ready = sem("root_ready")
        chan_ready = sem("chan_ready")
        blocks_cleared = sem("blocks_cleared")
        w_loaded = [sem(f"w_loaded{s}") for s in range(XSLOTS)]
        blocks_ready = sem("blocks_ready")
        mix_done = sem("mix_done")
        mix_banks = sem("mix_banks")
        mixed_stored = [sem(f"mixed_stored{m}") for m in range(4)]
        modes_loaded = sem("modes_loaded")
        shifts_summed = sem("shifts_summed")
        correction_ready = sem("correction_ready")
        peak_ready = sem("peak_ready")
        peak_stored = sem("peak_stored")
        peaks_loaded = sem("peaks_loaded")
        scale_ready = sem("scale_ready")
        weights_ready = sem("weights_ready")
        prep_step = sem("prep_step")
        ih_done = sem("ih_done")
        modes_picked = sem("modes_picked")
        hi_copied = sem("hi_copied")
        lo_copied = sem("lo_copied")
        x2_loaded = [sem(f"x2_loaded{s}") for s in range(OSLOTS)]
        xt_done = sem("xt_done")
        xt_banks = sem("xt_banks")
        z_done = sem("z_done")
        z_banks = sem("z_banks")
        added = sem("added")
        stored = [sem(f"stored{s}") for s in range(OSLOTS)]

        block = ctx.enter_context(nc.Block())

        @block.sync
        def _(sp):
            sp.dma_start(const[:, :], table).then_inc(consts_loaded, 16)

            def load_x(s, row, loaded):
                for part in range(2):
                    sp.dma_start(x_slot[s][:, HALF * part:HALF * (part + 1), :],
                                 x_rows[:, ds(row + HALF * part, HALF), :]).then_inc(loaded[s], 16)

            for s in range(XSLOTS):
                load_x(s, s * CHUNK, x1_loaded)
            for s in range(4):
                sp.dma_start(spare[0:1, s:s + 1], table[0:1, 0:1]).then_inc(stored[s], 16)
                sp.dma_start(spare[0:1, 4 + s:5 + s], table[0:1, 0:1]).then_inc(mixed_stored[s], 16)
            sp.wait_ge(w_cleared, 1)
            for b in range(2):
                sp.dma_start(w_block[b * C:(b + 1) * C, b * C:(b + 1) * C], res_w).then_inc(res_loaded, 16)
            sp.dma_start(bias[0:1, 0:C], res_b.rearrange("(a o) -> a o", a=1)).then_inc(res_loaded, 16)

            def refill(n, macro):
                chunks = sp.snap(CHUNKS * n + PER_MACRO * (macro + 1))
                sp.wait_ge(stats_done, chunks)
                sp.wait_ge(fw_done, chunks)
                for j in range(PER_MACRO):
                    s = (macro % 2) * PER_MACRO + j
                    load_x(s, R * n + STATROWS * (macro + 2) + CHUNK * j, x1_loaded)

            with sp.Fori(0, N - 1) as n:
                for macro in range(MACROS):
                    refill(n, macro)
            for macro in range(MACROS - 2):
                refill(N - 1, macro)

            def load_weights(s, it):
                rows = w0_rows if s < 4 else w1_rows
                for part in range(2):
                    sp.dma_start(ring[:, s, part * CELL // 2:(part + 1) * CELL // 2].rearrange(
                                     "p (a q f) -> p a q f", a=1, f=2 * C),
                                 rows[:, ds(4 * it + s % 4, 1), part * KP // 2:(part + 1) * KP // 2, :]
                                 ).then_inc(w_loaded[s], 16)

            for macro in range(2):
                sp.wait_ge(stats_done, CHUNKS * (N - 1) + PER_MACRO * (MACROS - 1 + macro))
                sp.wait_ge(fw_done, CHUNKS * (N - 1) + PER_MACRO * (MACROS - 1 + macro))
                for s in range(4 * macro, 4 * macro + 4):
                    load_weights(s, 0)
            with sp.Fori(0, 7) as it:
                for s in range(XSLOTS):
                    sp.wait_ge(mix_done, 4 + 8 * it + s + 1)
                    load_weights(s, it + 1)

            for s in range(OSLOTS):
                sp.wait_ge(mix_done, 4 + KH - 8 + s + 1)
                if s == 1:
                    sp.wait_ge(peaks_loaded, 16)
                load_x(s, s * CHUNK, x2_loaded)
            with sp.Fori(0, N * CHUNKS // OSLOTS - 1) as four:
                for s in range(OSLOTS):
                    sp.wait_ge(added, OSLOTS * four + s + 1)
                    load_x(s, CHUNK * (OSLOTS * four + s + OSLOTS), x2_loaded)
                    sp.dma_start(out_rows[:, ds(CHUNK * (OSLOTS * four + s), CHUNK), :], o_slot[s]
                                 ).then_inc(stored[s], 16)
            last = N * CHUNKS - OSLOTS
            for s in range(OSLOTS):
                sp.wait_ge(added, last + s + 1)
                sp.dma_start(out_rows[:, CHUNK * (last + s):CHUNK * (last + s + 1), :], o_slot[s]
                             ).then_inc(stored[s], 16)
            for s in range(OSLOTS):
                sp.wait_ge(stored[s], 16 * (N * CHUNKS // OSLOTS + 1))

        @block.gpsimd
        def _(pool):
            pool.memset(w_block[:, :], 0.0).then_inc(w_cleared, 1)
            pool.memset(ones[:, :], 1.0).then_inc(ones_set, 1)
            for m in range(4):
                pool.wait_ge(mixed_stored[m], 16 * 9)

            def load_modes(n):
                for ri in range(2):
                    pool.dma_start(modes[ri * KH:(ri + 1) * KH].rearrange("p (g t) o -> p g (t o)", t=4),
                                   mixed_out[n, ri]).then_inc(modes_loaded, 16)

            load_modes(0)
            with pool.Fori(0, N - 1) as n:
                pool.wait_ge(ih_done, AFILLS * (n + 1))
                load_modes(n + 1)

        @block.scalar
        def _(act):
            act.wait_ge(consts_loaded, 16)
            nc.scalar.copy(spare[:, 8:9], const[:, 0:1]).then_inc(mix_banks, 4)
            nc.scalar.copy(spare[:, 9:10], const[:, 0:1]).then_inc(z_banks, 2)

            def copy_rows_w(n, k):
                act.wait_ge(fw_done, CHUNKS * n + k + 1)
                nc.scalar.copy(rows_w[:, :, HALF * k:HALF * (k + 1)],
                               psum[:, k % 2, :].rearrange("p (h c) -> p c h", c=C)).then_inc(rows_w_copied, 1)

            def copy_rows_h(n):
                for f in range(FILLS):
                    act.wait_ge(turned, FILLS * n + f + 1)
                    nc.scalar.copy(rows_h[:, :, 4 * f:4 * f + 4],
                                   psum[:, TURN_BANKS[f % 4], :].rearrange("p (c m) -> p m c", c=4)).then_inc(rows_h_copied, 1)

            def take_root(n):
                act.wait_ge(var_ready, n + 1)
                nc.scalar.activation(root[:, :], var[:, :], ACT.Sqrt).then_inc(root_ready, 1)

            def copy_spectrum(n, b):
                act.wait_ge(fh_done, 4 * n + b + 1)
                act.wait_ge(chan_ready, n + 1)
                nc.scalar.activation(spectrum[:, :, 4 * b:4 * b + 4, ds(n, 1), :].rearrange("p k q n r -> p q (n r) k"),
                                     psum[:, 4 + b, :].rearrange("p (q r k) -> p q r k", q=4, r=2),
                                     ACT.Identity, scale=chan[:, 0:1]).then_inc(spectrum_copied, 1)

            for k in range(CHUNKS):
                copy_rows_w(0, k)
            copy_rows_h(0)
            with act.Fori(0, N - 1) as n:
                for k in range(CHUNKS):
                    copy_rows_w(n + 1, k)
                    if k == ROOT_AT:
                        take_root(n)
                    if k in SPECTRUM_AT:
                        copy_spectrum(n, SPECTRUM_AT.index(k))
                copy_rows_h(n + 1)
            take_root(N - 1)
            for b in range(4):
                copy_spectrum(N - 1, b)

            def mix_copy(it, m):
                act.wait_ge(mix_done, 4 + 8 * it + 2 * m + 2)
                act.wait_ge(mixed_stored[m], 16 * (it + 1))
                nc.scalar.copy(mix_out[:, m, :, :], psum[:, m, :].rearrange("p (k f) -> p k f", k=2)
                               ).then_inc(mix_banks, 1)
                act.wait_ge(mix_banks, 4 + 4 * it + m + 1)
                kh = 4 * it + 2 * m if m < 2 else 4 * it + MODE + 2 * (m - 2)
                act.dma_start(mixed_in[:, ds(kh, 2), :], mix_out[:, m, :, :]).then_inc(mixed_stored[m], 16)

            with act.Fori(0, 8) as it:
                for m in range(4):
                    mix_copy(it, m)

            def silu(n, cur, it, v):
                unit = UNITS * n + 8 * it + v
                s = v // 2
                if v % 2 == 0:
                    act.wait_ge(stored[s], 16 * (4 * n + it + 1))
                act.wait_ge(z_done, unit + 1)
                bank = 2 * (v % 2)
                nc.scalar.activation(
                    o_slot[s][:, HALF * (v % 2):HALF * (v % 2 + 1), :],
                    psum[:, bank:bank + 2, :].rearrange("p b (h f) -> p (b h) f", f=ROW),
                    ACT.Silu, scale=span[:, S_UNZ + cur:S_UNZ + cur + 1]).then_inc(z_banks, 1)

            def pick_modes(n, it, f, count):
                act.wait_ge(peak_ready, n + 1)
                nc.scalar.copy(
                    picked_modes[:, :, 0:2 * count, :],
                    modes.rearrange("p k (half o) -> p half o k", half=2)[:, :, ds(2 * f, 2 * count), :]
                ).then_inc(modes_picked, 1)

            def copy_hi(n, cur, f, bank):
                act.wait_ge(scale_ready, n + 1)
                act.wait_ge(ih_done, AFILLS * n + f + 1)
                for half in range(2):
                    rows = slice(C * half, C * (half + 1))
                    ins = nc.scalar.activation(rows_back[cur][rows, :, ds(32 * half + 2 * f, 2)],
                                               psum[rows, bank, :].rearrange("p (o h) -> p h o", o=2),
                                               ACT.Identity, scale=span[rows, S_H:S_H + 1])
                ins.then_inc(hi_copied, 1)

            def store_peak(n):
                act.wait_ge(peak_ready, n + 1)
                act.dma_start(peaks_dram, span[:, S_PEAK:S_PEAK + 1]).then_inc(peak_stored, 16)

            def load_peaks(n):
                act.wait_ge(peak_stored, 16 * (n + 1))
                act.dma_start(peaks, peaks_dram.rearrange("p a -> (p a)").partition_broadcast(P)
                              ).then_inc(peaks_loaded, 16)

            def first_round(n, cur, ahead=True):
                for v in range(8):
                    silu(n, cur, 0, v)
                    if ahead and v == 4:
                        store_peak(n + 1)
                    if ahead and v == 5:
                        load_peaks(n + 1)
                    if ahead and v == 5:
                        pick_modes(n + 1, 0, 0, 1)
                    if ahead and v == FIRST_AT:
                        copy_hi(n + 1, 1 - cur, 0, AHEAD_BANK)

            def round_of_units(n, cur, it, ahead=True):
                if ahead:
                    pick_modes(n + 1, it, PIECE * it - PIECE + 1, PIECE)
                for v in range(8):
                    silu(n, cur, it, v)
                    if ahead and v in AHEAD_AT:
                        j = AHEAD_AT.index(v)
                        copy_hi(n + 1, 1 - cur, PIECE * it - PIECE + 1 + j, AHEAD_BANK + j % 2)

            def image(n, cur, ahead=True):
                first_round(n, cur, ahead)
                with act.Fori(1, 4) as it:
                    round_of_units(n, cur, it, ahead)

            store_peak(0)
            load_peaks(0)
            for f in range(AFILLS):
                copy_hi(0, 0, f, FIRST_BANKS[f % len(FIRST_BANKS)])
            with act.Fori(0, N // 2 - 1) as pair:
                image(2 * pair, 0)
                image(2 * pair + 1, 1)
            image(N - 2, 0)
            image(N - 1, 1, ahead=False)

        @block.vector
        def _(dve):
            dve.wait_ge(consts_loaded, 16)
            nc.vector.tensor_copy(ew[:, 0, :, :], ew_full).then_inc(prep_step, 1)
            dve.wait_ge(prep_step, 1)
            nc.vector.tensor_tensor(ew[:, 1, :, :], ew_full, ew[:, 0, :, :], ALU.subtract).then_inc(prep_step, 1)

            steps = [0]
            STEPS = 14

            def step(n, ins):
                steps[0] += 1
                ins.then_inc(dve_step, 1)
                dve.wait_ge(dve_step, STEPS * n + steps[0])

            means = cells[:, :, :, 1:5:3]
            moments = cells[:, :, :, 2:6:3]

            def measure(n, macro, target):
                for j in range(PER_MACRO):
                    dve.wait_ge(x1_loaded[(macro % 2) * PER_MACRO + j], 32 * (2 * n + macro // 2 + 1))
                s = (macro % 2) * PER_MACRO
                rows = ring[:, s:s + PER_MACRO, :].rearrange("p s (h two c) -> p (s h) two c", two=2, c=C)
                for g in range(GROUPS):
                    ins = nc.vector.bn_stats(target[:, g, :], rows[:, :, :, 2 * g:2 * g + 2])
                ins.then_inc(stats_done, PER_MACRO)

            def sum_means(n):
                dve.wait_ge(stats_done, CHUNKS * (n + 1))
                nc.vector.tensor_reduce(sums[:, :], means.rearrange("p m g s -> p g m s"), AX.XY, ALU.add
                                        ).then_inc(sums_ready, 1)

            def sum_squares(n):
                steps[0] = 0
                dve.wait_ge(totals_ready, 2 * n + 1)
                step(n, nc.vector.tensor_scalar(mean[:, :], psum[:, 2, 0:GROUPS],
                                                1.0 / (P * MACROS * 2), None, ALU.mult))
                step(n, nc.vector.tensor_tensor(
                    spread[:, :, :, :], means,
                    mean[:, :].rearrange("p (a g b) -> p a g b", a=1, b=1).to_broadcast([P, MACROS, GROUPS, 2]),
                    ALU.subtract))
                step(n, nc.vector.tensor_tensor(spread[:, :, :, :], spread[:, :, :, :], spread[:, :, :, :], ALU.mult))
                step(n, nc.vector.scalar_tensor_tensor(spread[:, :, :, :], spread[:, :, :, :],
                                                       float(STATROWS * 2), moments, ALU.mult, ALU.add))
                nc.vector.tensor_reduce(sums[:, :], spread[:, :, :, :].rearrange("p m g s -> p g m s"), AX.XY, ALU.add
                                        ).then_inc(sums_ready, 1)

            def find_var(n):
                dve.wait_ge(totals_ready, 2 * n + 2)
                nc.vector.tensor_scalar(var[:, :], psum[:, 3, 0:GROUPS], 1.0 / (R * R * (C // GROUPS)), EPS,
                                        ALU.mult, ALU.add).then_inc(var_ready, 1)

            def find_scale_of_image(n):
                dve.wait_ge(root_ready, n + 1)
                step(n, nc.vector.reciprocal(rstd[:, :], root[:, :]))
                step(n, nc.vector.tensor_tensor(root[:, :], rstd[:, :], rstd[:, :], ALU.mult))
                step(n, nc.vector.tensor_tensor(root[:, :], root[:, :], var[:, :], ALU.mult))
                step(n, nc.vector.tensor_scalar(root[:, :], root[:, :], -0.5, 1.5, ALU.mult, ALU.add))
                step(n, nc.vector.tensor_tensor(rstd[:, :], rstd[:, :], root[:, :], ALU.mult))
                step(n, nc.vector.tensor_tensor(picked[:, :], rstd[:, :], mask, ALU.mult))
                step(n, nc.vector.tensor_reduce(chan[:, 0:1], picked[:, :], AX.X, ALU.add))
                step(n, nc.vector.tensor_tensor(picked[:, :], mean[:, :], mask, ALU.mult))
                step(n, nc.vector.tensor_reduce(chan[:, 1:2], picked[:, :], AX.X, ALU.add))
                step(n, nc.vector.tensor_tensor(chan[:, 2:3], chan[:, 0:1], chan[:, 1:2], ALU.mult))
                nc.vector.tensor_scalar(scale_all[:, ds(n, 1)], chan[:, 0:1], 1.0, None, ALU.mult)
                nc.vector.tensor_scalar(shift_all[:, ds(n, 1)], chan[:, 2:3], 1.0, None, ALU.mult)
                nc.vector.tensor_scalar(dc_all[:, ds(n, 1)], chan[:, 2:3], -float(R), None, ALU.mult
                                        ).then_inc(chan_ready, 1)
                assert steps[0] == STEPS

            for macro in range(MACROS):
                measure(0, macro, cells[:, macro])
            with dve.Fori(0, N - 1) as n:
                sum_means(n)
                measure(n + 1, 0, early)
                sum_squares(n)
                dve.wait_ge(stats_done, CHUNKS * (n + 1) + PER_MACRO)
                nc.vector.tensor_scalar(cells[:, 0, :, :], early[:, :, :], 1.0, None, ALU.mult)
                measure(n + 1, 1, cells[:, 1])
                find_var(n)
                measure(n + 1, 2, cells[:, 2])
                find_scale_of_image(n)
                measure(n + 1, 3, cells[:, 3])
            sum_means(N - 1)
            sum_squares(N - 1)
            find_var(N - 1)
            find_scale_of_image(N - 1)

            dve.wait_ge(turned, FILLS * N)
            nc.vector.memset(blocks.rearrange("p b q v k n r -> p (b q v k n r)"), 0.0).then_inc(blocks_cleared, 1)
            dve.wait_ge(spectrum_copied, 4 * N)
            nc.vector.tensor_tensor(spectrum[0:C, 0, 0, :, 0], spectrum[0:C, 0, 0, :, 0], dc_all[0:C, :], ALU.add
                                    ).then_inc(blocks_cleared, 1)
            dve.wait_ge(blocks_cleared, 2)
            with dve.Fori(0, 8) as it:
                for s in range(8):
                    dve.wait_ge(mix_done, 8 * it + s + 1)
                    kh = 4 * it + s if s < 4 else 4 * it + MODE + s - 4
                    for half in range(2):
                        rows = slice(C * half, C * (half + 1))
                        z = spectrum[rows, kh, :, :, :]
                        b = blocks[rows, s % 4, :, :, half, :, :]
                        nc.vector.tensor_scalar(b[:, :, 0], z, 1.0, None, ALU.mult)
                        nc.vector.tensor_scalar(b[:, :, 1, :, 0], z[:, :, :, 1], -1.0, None, ALU.mult)
                        ins = nc.vector.tensor_scalar(b[:, :, 1, :, 1], z[:, :, :, 0], 1.0, None, ALU.mult)
                    ins.then_inc(blocks_ready, 1)

            def xt_copy(n, it, v):
                dve.wait_ge(xt_done, UNITS * n + 8 * it + v + 1)
                nc.vector.tensor_copy(xt[v % 2].rearrange("p (b f) -> p b f", b=2), psum[:, 4:6, :]
                                      ).then_inc(xt_banks, 1)

            def add_x(n, it, v):
                dve.wait_ge(z_banks, UNITS * n + 8 * it + v + 3)
                rows = slice(HALF * (v % 2), HALF * (v % 2 + 1))
                s = v // 2
                ins = nc.vector.tensor_tensor(o_slot[s][:, rows, :], o_slot[s][:, rows, :], x_slot[s][:, rows, :],
                                              ALU.add)
                if v % 2:
                    ins.then_inc(added, 1)

            PREP = 11
            prepared = [0]

            def prep(n, ins):
                prepared[0] += 1
                ins.then_inc(prep_step, 1)
                dve.wait_ge(prep_step, 2 + PREP * n + prepared[0])

            def col(k):
                return span[:, k:k + 1]

            def find_peak(n):
                prepared[0] = 0
                dve.wait_ge(modes_loaded, 32 * (n + 1))
                prep(n, nc.vector.tensor_tensor(modes[0:1, 0:1, :], modes[0:1, 0:1, :], correction[:, ds(n, 1), :],
                                                ALU.add))
                prep(n, nc.vector.tensor_reduce(col(S_HALF), modes[:, 0:KW // 2, :].rearrange("p k o -> p (k o)"), AX.X,
                                                ALU.max, apply_absolute_value=True))

            def finish_peak(n):
                prep(n, nc.vector.tensor_reduce(col(S_TOP), modes[:, KW // 2:, :].rearrange("p k o -> p (k o)"), AX.X,
                                                ALU.max, apply_absolute_value=True))
                nc.vector.tensor_tensor(col(S_PEAK), col(S_TOP), col(S_HALF), ALU.max).then_inc(peak_ready, 1)

            def find_scale(n, cur):
                dve.wait_ge(peaks_loaded, 16 * (n + 1))
                prep(n, nc.vector.tensor_reduce(col(S_TOP), peaks, AX.X, ALU.max))
                prep(n, nc.vector.tensor_scalar(col(S_TOP), col(S_TOP), TINY, None, ALU.max))
                prep(n, nc.vector.reciprocal(col(S_INV), col(S_TOP)))
                prep(n, nc.vector.tensor_scalar(col(S_POW).bitcast(int32), col(S_INV).bitcast(int32), POWER_BITS, None,
                                                ALU.bitwise_and))
                prep(n, nc.vector.tensor_scalar(col(S_Z), col(S_POW), H_SCALE * E_SCALE, None, ALU.mult))
                prep(n, nc.vector.reciprocal(col(S_UNZ + cur), col(S_Z)))
                nc.vector.tensor_scalar(col(S_H), col(S_POW), H_SCALE, None, ALU.mult).then_inc(scale_ready, 1)

            def scale_weights(n, cur):
                prep(n, nc.vector.tensor_scalar(col(S_CHAN), scale_all[:, ds(n, 1)], 1.0, None, ALU.mult))
                prep(n, nc.vector.tensor_scalar(col(S_W), col(S_CHAN), col(S_Z), None, ALU.mult))
                nc.vector.tensor_scalar(w_scaled[:, cur, :], w_block[:, :], col(S_W), None, ALU.mult
                                        ).then_inc(weights_ready, 1)
                assert prepared[0] == PREP

            def copy_lo(n, cur, f, bank):
                dve.wait_ge(hi_copied, AFILLS * n + f + 1)
                for half in range(2):
                    rows = slice(C * half, C * (half + 1))
                    other = slice(C * (1 - half), C * (2 - half))
                    ins = nc.vector.scalar_tensor_tensor(
                        rows_back[cur][other, :, ds(32 * half + 2 * f, 2)],
                        psum[rows, bank, :].rearrange("p (o h) -> p h o", o=2), span[rows, S_H:S_H + 1],
                        rows_back[cur][rows, :, ds(32 * half + 2 * f, 2)], ALU.mult, ALU.subtract)
                ins.then_inc(lo_copied, 1)

            def first_round(n, cur, ahead=True):
                for v in range(8):
                    xt_copy(n, 0, v + 1) if v < 7 else xt_copy(n, 1, 0)
                    if ahead and v == FIRST_AT + 1:
                        copy_lo(n + 1, 1 - cur, 0, AHEAD_BANK)
                    add_x(n, 0, v)
                    if ahead and v == 2:
                        find_peak(n + 1)
                    if ahead and v == 3:
                        finish_peak(n + 1)
                    if ahead and v == 6:
                        find_scale(n + 1, 1 - cur)
                    if ahead and v == 7:
                        scale_weights(n + 1, 1 - cur)

            def round_of_units(n, cur, it, ahead=True, last=False):
                for v in range(8):
                    if not (last and v == 7):
                        xt_copy(n, it, v + 1) if v < 7 else xt_copy(n, it + 1, 0)
                    if ahead and v - 1 in AHEAD_AT:
                        j = AHEAD_AT.index(v - 1)
                        copy_lo(n + 1, 1 - cur, PIECE * it - PIECE + 1 + j, AHEAD_BANK + j % 2)
                    add_x(n, it, v)

            def image(n, cur):
                first_round(n, cur)
                with dve.Fori(1, 4) as it:
                    round_of_units(n, cur, it)

            dve.wait_ge(res_loaded, 48)
            nc.vector.tensor_scalar(bias[0:1, 0:C], bias[0:1, 0:C], float(R), None, ALU.mult).then_inc(xt_banks, 2)
            dve.wait_ge(xt_banks, 2)
            dve.wait_ge(shifts_summed, N)
            nc.vector.scalar_tensor_tensor(
                correction, psum[0:1, 4, :].rearrange("p (n o) -> p n o", o=C), -float(R),
                bias[0:1, 0:C].rearrange("p (a o) -> p a o", a=1).to_broadcast([1, N, C]), ALU.mult, ALU.add
            ).then_inc(correction_ready, 1)
            dve.wait_ge(correction_ready, 1)
            find_peak(0)
            finish_peak(0)
            xt_copy(0, 0, 0)
            find_scale(0, 0)
            for f in range(AFILLS):
                copy_lo(0, 0, f, FIRST_BANKS[f % len(FIRST_BANKS)])
            scale_weights(0, 0)
            with dve.Fori(0, N // 2 - 1) as pair:
                image(2 * pair, 0)
                image(2 * pair + 1, 1)
            image(N - 2, 0)
            first_round(N - 1, 1, ahead=False)
            with dve.Fori(1, 3) as it:
                round_of_units(N - 1, 1, it, ahead=False)
            round_of_units(N - 1, 1, 3, ahead=False, last=True)

        @block.tensor
        def _(pe):
            pe.wait_ge(consts_loaded, 16)
            pe.wait_ge(ones_set, 1)
            nc.tensor.matmul(psum[:, 0, 0:P], ones[:, :], ones[:, :], start=True, stop=True).then_inc(mix_done, 4)

            def total(n, which):
                pe.wait_ge(sums_ready, 2 * n + which + 1)
                nc.tensor.matmul(psum[:, 2 + which, 0:GROUPS], ones[:, :], sums[:, :], start=True, stop=True
                                 ).then_inc(totals_ready, 1)

            def along_w(n, k):
                if k >= 2:
                    pe.wait_ge(rows_w_copied, CHUNKS * n + k - 1)
                pe.wait_ge(x1_loaded[k % XSLOTS], 32 * (2 * n + k // XSLOTS + 1))
                for two in range(2):
                    for half in range(2):
                        ins = nc.tensor.matmul(
                            psum[half * C:(half + 1) * C, k % 2, :], fw[:, two, :],
                            x_slot[k % XSLOTS][:, HALF * half:HALF * (half + 1), two * C:(two + 1) * C],
                            start=two == 0, stop=two == 1)
                ins.then_inc(fw_done, 1)

            def turn(n):
                pe.wait_ge(rows_w_copied, CHUNKS * (n + 1))
                for f in range(FILLS):
                    if f >= 4:
                        pe.wait_ge(rows_h_copied, FILLS * n + f - 3)
                    for c in range(4):
                        ins = nc.tensor.transpose(psum[:, TURN_BANKS[f % 4], c * P:(c + 1) * P], rows_w[:, 4 * f + c, :], ident)
                    ins.then_inc(turned, 1)

            def along_h(n, q):
                if q == 0:
                    pe.wait_ge(rows_h_copied, FILLS * (n + 1))
                for half in range(2):
                    for ri in range(2):
                        for odd in range(2):
                            m = half * 2 * KW + ri * KW + 2 * q + odd
                            ins = nc.tensor.matmul(psum[odd * C:(odd + 1) * C, 4 + q // 4, (q % 4) * P:(q % 4 + 1) * P],
                                                   rows_h[:, m, :], gh[:, half, ri, :],
                                                   start=(half, ri) == (0, 0), stop=(half, ri) == (1, 1))
                if q % 4 == 3:
                    ins.then_inc(fh_done, 1)
                if q in (1, 2):
                    total(n, q - 1)

            for k in range(CHUNKS):
                along_w(0, k)
            turn(0)
            with pe.Fori(0, N - 1) as n:
                for k in range(CHUNKS):
                    if k < 2:
                        pe.wait_ge(rows_h_copied, FILLS * (n + 1) - 3 + k)
                    along_w(n + 1, k)
                    along_h(n, k)
                pe.wait_ge(chan_ready, n + 1)
                turn(n + 1)
            for q in range(KP):
                along_h(N - 1, q)

            pe.wait_ge(chan_ready, N)
            pe.wait_ge(spectrum_copied, 4 * N)
            pe.wait_ge(res_loaded, 48)
            for n in range(N):
                nc.tensor.matmul(psum[0:1, 4, n * C:(n + 1) * C], shift_all[:, n:n + 1], w_block[:, 0:C],
                                 start=True, stop=True).then_inc(shifts_summed, 1)

            with pe.Fori(0, 8) as it:
                for s in range(8):
                    pe.wait_ge(blocks_ready, 8 * it + s + 1)
                    pe.wait_ge(w_loaded[s], 32 * (it + 1))
                    if s % 2 == 0:
                        pe.wait_ge(mix_banks, 4 * it + s // 2 + 1)
                    for t in range(4):
                        for v in range(2):
                            for g in range(4):
                                ins = nc.tensor.matmul(
                                    psum[32 * g:32 * (g + 1), s // 2, (4 * (s % 2) + t) * C:(4 * (s % 2) + t + 1) * C],
                                    blocks[:, s % 4, 4 * t + g, v, :, :, :].rearrange("p k n r -> p (k n r)"), w_slot[s][:, 4 * t + g, :, v],
                                    start=v == 0, stop=v == 1)
                    ins.then_inc(mix_done, 1)

            def transpose_x(n, it, v):
                s = v // 2
                if v % 2 == 0:
                    pe.wait_ge(x2_loaded[s], 32 * (4 * n + it + 1))
                pe.wait_ge(xt_banks, UNITS * n + 8 * it + v + 2)
                for row in range(HALF):
                    ins = nc.tensor.transpose(psum[:, 4 + row // 4, (row % 4) * P:(row % 4 + 1) * P],
                                              x_slot[s][:, HALF * (v % 2) + row, :], ident)
                ins.then_inc(xt_done, 1)

            def sum_unit(n, cur, it, v):
                pe.wait_ge(xt_banks, UNITS * n + 8 * it + v + 3)
                pe.wait_ge(z_banks, UNITS * n + 8 * it + v + 1)
                if v == 0:
                    pe.wait_ge(weights_ready, n + 1)
                    pe.wait_ge(hi_copied, AFILLS * (n + 1))
                    pe.wait_ge(lo_copied, AFILLS * (n + 1))
                for four in range(2):
                    row = HALF * (8 * it + v) + 4 * four
                    z = psum[:, 2 * (v % 2) + four, :].rearrange("p (h two o) -> p h two o", two=2, o=C)
                    for two in range(2):
                        for part in range(2):
                            nc.tensor.matmul(z[:, :, two, :], ew[:, part, two, :], rows_back[cur][:, ds(row, 4), :],
                                             start=(two, part) == (0, 0), stop=False, skip_group_check=True)
                    for h in range(4):
                        c0 = (4 * four + h) * P
                        ins = nc.tensor.matmul(z[:, h, :, :], xt[v % 2][:, c0:c0 + P], w_scaled[:, cur, :],
                                               start=False, stop=h == 3, skip_group_check=True)
                ins.then_inc(z_done, 1)

            def along_h_back(bank, of_channel):
                for o in range(2):
                    for half in range(2):
                        for ri in range(2):
                            tile = 2 * half + ri
                            ins = nc.tensor.matmul(psum[32 * tile:32 * (tile + 1), bank, o * R:(o + 1) * R],
                                                   of_channel(half, o), eh[:, ri, :], start=True, stop=True)
                ins.then_inc(ih_done, 1)

            def one_ahead(n, it, f, j):
                if j == 0:
                    pe.wait_ge(modes_picked, 4 * n + it - 3)
                pe.wait_ge(lo_copied, AFILLS * n + f - (j > 0))
                along_h_back(AHEAD_BANK + j % 2, lambda half, o: picked_modes[:, half, 2 * j + o, :])

            def first_round(n, cur, ahead=True):
                for v in range(8):
                    transpose_x(n, 0, v + 1) if v < 7 else transpose_x(n, 1, 0)
                    sum_unit(n, cur, 0, v)
                    if ahead and v == FIRST_AT:
                        one_ahead(n + 1, 0, 0, 0)

            def round_of_units(n, cur, it, ahead=True, last=False):
                for v in range(8):
                    if not (last and v == 7):
                        transpose_x(n, it, v + 1) if v < 7 else transpose_x(n, it + 1, 0)
                    sum_unit(n, cur, it, v)
                    if ahead and v in AHEAD_AT:
                        j = AHEAD_AT.index(v)
                        one_ahead(n + 1, it, PIECE * it - PIECE + 1 + j, j)

            def image(n, cur):
                first_round(n, cur)
                with pe.Fori(1, 4) as it:
                    round_of_units(n, cur, it)

            pe.wait_ge(mix_banks, 4 + 4 * 8)
            pe.wait_ge(correction_ready, 1)
            pe.wait_ge(prep_step, 2)
            transpose_x(0, 0, 0)
            pe.wait_ge(peak_ready, 1)
            for f in range(AFILLS):
                if f >= len(FIRST_BANKS):
                    pe.wait_ge(lo_copied, f - len(FIRST_BANKS) + 1)
                along_h_back(FIRST_BANKS[f % len(FIRST_BANKS)], lambda half, o: modes[:, :, 32 * half + 2 * f + o])
            with pe.Fori(0, N // 2 - 1) as pair:
                image(2 * pair, 0)
                image(2 * pair + 1, 1)
            image(N - 2, 0)
            first_round(N - 1, 1, ahead=False)
            with pe.Fori(1, 3) as it:
                round_of_units(N - 1, 1, it, ahead=False)
            round_of_units(N - 1, 1, 3, ahead=False, last=True)


def kernel(x, L0_conv_w0, L0_conv_w1, L0_conv_res_w, L0_conv_res_b):
    import concourse.bacc as bacc
    from concourse.bass_utils import run_bass_kernel_spmd

    nc = bacc.Bacc("TRN2", target_bir_lowering=False, num_devices=1)
    arrays, args = {}, []
    for name, a in (("x", x), ("w0", L0_conv_w0), ("w1", L0_conv_w1), ("res_w", L0_conv_res_w),
                    ("res_b", L0_conv_res_b), ("table", constant_table())):
        a = np.ascontiguousarray(a)
        arrays[name] = a
        args.append(nc.dram_tensor(name, a.shape, mybir.dt.from_np(a.dtype), kind="ExternalInput").ap())
    out = nc.dram_tensor("out", (N, R, R, C), mybir.dt.float32, kind="ExternalOutput").ap()
    spectral_layer(nc, *args, out)
    return run_bass_kernel_spmd(nc, [arrays], core_ids=[0]).results[0]["out"]
```
